# Optimizing a Trainium2 kernel written in Bass

```python
import numpy as np
import jax
import jax.numpy as jnp

def _softmax(x, axis=-1):
    return jax.nn.softmax(x, axis=axis)

def _gelu(x):
    return jax.nn.gelu(x, approximate=True)

def _silu(x):
    return jax.nn.silu(x)

def _sigmoid(x):
    return jax.nn.sigmoid(x)

def _layernorm(x, axis=-1, eps=1e-05):
    m = jnp.mean(x, axis=axis, keepdims=True)
    v = jnp.var(x, axis=axis, keepdims=True)
    return (x - m) / jnp.sqrt(v + eps)

def _scatter_add(tgt, idx, src, axis=0):
    return tgt.at[idx].add(src)

def _segment_sum(src, seg, n):
    return jax.ops.segment_sum(src, seg, n)
kernel_name = 'mk_conv_preact_d1_conv_nchw384_r2_1af4f1'

def setup_inputs(seed: int=0):
    np.random.seed(seed)
    _w = jnp.asarray

    def _rec_inputs():
        import jax
        import jax.numpy as jnp
        _gk = jax.random.key(seed)
        x = -0.0003483 + 1 * jax.random.normal(jax.random.fold_in(_gk, 1), (16, 192, 48, 48), jnp.float32)
        return x
    x = _rec_inputs()

    def _L0_conv_setup():
        import jax, jax.numpy as jnp
        import numpy as np
        EPS = 1e-12
        key = jax.random.key(seed)
        k1, k2, k3 = jax.random.split(key, 3)
        b, c, H, W = (16, 192, 48, 48)
        heads = 8
        x = jax.random.normal(k1, (b, c, H, W), dtype=jnp.float32)
        w_qkv = jax.random.normal(k2, (c, 3 * c), dtype=jnp.float32) / np.sqrt(c)
        temperature = jnp.ones((1, heads, 1, 1), dtype=jnp.float32)
        w_out = jax.random.normal(k3, (c, c), dtype=jnp.float32) / np.sqrt(c)
        b_out = jnp.zeros((c,), dtype=jnp.float32)
        return {'x': x, 'w_qkv': w_qkv, 'temperature': temperature, 'w_out': w_out, 'b_out': b_out}
    _L0_conv_all = _L0_conv_setup()
    _L0_conv_in = {k: v for k, v in _L0_conv_all.items() if k in ('w_qkv', 'temperature', 'w_out', 'b_out')}
    del _L0_conv_all
    return {'x': x, 'L0_conv_w_qkv': _L0_conv_in['w_qkv'], 'L0_conv_temperature': _L0_conv_in['temperature'], 'L0_conv_w_out': _L0_conv_in['w_out'], 'L0_conv_b_out': _L0_conv_in['b_out']}

def reference(x, L0_conv_w_qkv, L0_conv_temperature, L0_conv_w_out, L0_conv_b_out):
    import jax
    import jax.numpy as jnp

    def _L0_conv_ref(x, w_qkv, temperature, w_out, b_out):
        import jax, jax.numpy as jnp
        import numpy as np
        EPS = 1e-12
        b, c, H, W = x.shape
        h = temperature.shape[1]
        d = c // h
        n = H * W
        xt = x.reshape(b, c, n).transpose(0, 2, 1)
        qkv = xt @ w_qkv
        q, k, v = jnp.split(qkv, 3, axis=-1)
        q = q.reshape(b, n, h, d).transpose(0, 2, 1, 3)
        k = k.reshape(b, n, h, d).transpose(0, 2, 3, 1)
        v = v.reshape(b, n, h, d).transpose(0, 2, 1, 3)
        q = q / jnp.maximum(jnp.sqrt(jnp.sum(q * q, axis=-2, keepdims=True)), EPS)
        k = k / jnp.maximum(jnp.sqrt(jnp.sum(k * k, axis=-1, keepdims=True)), EPS)
        k = k * temperature
        attn = jnp.einsum('bhpn,bhnq->bhpq', k, q)
        attn = jax.nn.softmax(attn, axis=-1)
        out = jnp.einsum('bhnp,bhpq->bhnq', v, attn)
        out = out.transpose(0, 2, 1, 3).reshape(b, n, c)
        out = out @ w_out + b_out
        out = out.transpose(0, 2, 1).reshape(b, c, H, W)
        return out

    def _gn(v, G=32, eps=1e-05):
        B_, C_, H_, W_ = v.shape
        g = v.reshape(B_, G, C_ // G, H_, W_)
        m = jnp.mean(g, axis=(2, 3, 4), keepdims=True)
        s = jnp.var(g, axis=(2, 3, 4), keepdims=True)
        return ((g - m) / jnp.sqrt(s + eps)).reshape(v.shape)

    def _ln_c(v, eps=1e-06):
        m = jnp.mean(v, axis=1, keepdims=True)
        s = jnp.var(v, axis=1, keepdims=True)
        return (v - m) / jnp.sqrt(s + eps)

    def _ln_t(v, eps=1e-05):
        m = jnp.mean(v, axis=-1, keepdims=True)
        s = jnp.var(v, axis=-1, keepdims=True)
        return (v - m) / jnp.sqrt(s + eps)

    def _to_tokens(v):
        B_, C_, H_, W_ = v.shape
        return v.reshape(B_, C_, H_ * W_).transpose(0, 2, 1)

    def _from_tokens(t, like):
        B_, C_, H_, W_ = like.shape
        return t.transpose(0, 2, 1).reshape(B_, C_, H_, W_)
    x = x + _L0_conv_ref(_gn(x), L0_conv_w_qkv, L0_conv_temperature, L0_conv_w_out, L0_conv_b_out)
    return x

_drawn_inputs = setup_inputs


def setup_inputs(seed=0):
    import zlib

    import numpy as np

    out = dict(_drawn_inputs(seed))
    spreads = {'L0_conv_temperature': (1.0, 0.2), 'L0_conv_b_out': (0.0, 0.1)}
    factors = {}
    for name, (base, spread) in spreads.items():
        noise = np.random.default_rng([zlib.crc32(name.encode()), seed]).standard_normal(out[name].shape)
        drawn = base * np.exp(spread * noise) if base else spread * noise
        out[name] = jnp.asarray(drawn.astype(out[name].dtype))
    for name, factor in factors.items():
        out[name] = (out[name] * factor).astype(out[name].dtype)
    return out
```

```python
from contextlib import ExitStack

import numpy as np

import concourse.bass as bass
from concourse import mybir

ALU = mybir.AluOpType
ACT = mybir.ActivationFunctionType
F32 = mybir.dt.float32
F16 = mybir.dt.float16
BF16 = mybir.dt.bfloat16
AX_X = mybir.AxisListType.X

P = 128
HEADS = 8
CG = 6
GN_EPS = 1e-5
NORM_EPS = 1e-12
NX = 3
TOK_RING = 3
GN_COL = 400

X_SCALE = 1 / 8
M_SCALE = 8.0
W_SCALE = 16.0
A_SCALE = 16.0
NORM_FACTOR = W_SCALE * X_SCALE ** 2
LOGIT_FACTOR = NORM_FACTOR / (W_SCALE ** 2 * X_SCALE ** 2)
M_EVAC = M_SCALE / (W_SCALE ** 2 * A_SCALE)

G_C, G_HL, G_B = 192, 256, 448


def slot_is_vector(j):
    return j % 3 == 2


def preact_attention(nc, x, w_qkv, temperature, w_out, b_out, ident, groups, headmask, out):
    B, C, H, W = x.shape
    N = H * W
    D = C // HEADS
    C1 = C - P
    PAIRS = B // 2
    SLOTS = N // P
    HC = C // 2
    NH = HEADS // 2
    HALF = N // 2
    TILE = 3 * N
    BLOCKS = [(c, min(512, N - c)) for c in range(0, N, 512)]
    NB = len(BLOCKS)
    OUTS = [(t, c, w) for t in (0, 2, 1) for c, w in BLOCKS]
    NO = len(OUTS)
    NV = sum(slot_is_vector(j) for j in range(SLOTS))
    NA = SLOTS - NV
    CHUNKS = [(t, hf) for hf in (0, 1) for t in (0, 2, 1)]
    NC_ = len(CHUNKS)
    assert C == 192 and N % P == 0 and (2 * NO) % 2 == 0 and SLOTS % 6 == 0 and PAIRS % 2 == 0

    x_d = x.rearrange("b c h w -> b c (h w)")
    o_d = out.rearrange("b c h w -> b c (h w)")

    with ExitStack() as ctx:
        def sb(name, shape, dt=F32):
            return ctx.enter_context(nc.sbuf_tensor(name, shape, dt))

        def sem(name):
            return ctx.enter_context(nc.semaphore(name))

        x_sb = sb("x_sb", [P, NX * TILE])
        h_sb = sb("h_sb", [P, 2, 3, N], F16)
        l_sb = sb("l_sb", [P, 2, 3, N], F16)
        xn = sb("xn", [P, 2, HALF])
        tok = sb("tok", [P, TOK_RING, 2, 384], F16)
        w0 = sb("w0", [P, 3 * C])
        w1 = sb("w1", [P, 3 * C])
        wh0 = sb("wh0", [P, 2 * C], F16)
        wl0 = sb("wl0", [P, 2 * C], F16)
        wh1 = sb("wh1", [P, 2 * C], F16)
        wl1 = sb("wl1", [P, 2 * C], F16)
        wkh1 = sb("wkh1", [P, 2, C], F16)
        wkl1 = sb("wkl1", [P, 2, C], F16)
        wvh = sb("wvh", [HC, 2, C], F16)
        wvl = sb("wvl", [HC, 2, C], F16)
        woh = sb("woh", [HC, 2, C + P], F16)
        wol = sb("wol", [HC, 2, C + P], F16)
        id16 = sb("id16", [P, P], F16)
        grp = sb("grp", [P, 6, P], BF16)
        mask = sb("mask", [HC, HC])
        mask16 = sb("mask16", [HC, HC], F16)
        id32 = sb("id32", [HC, HC])
        ones = sb("ones", [P, 3], F16)
        minus_half = sb("minus_half", [P, 1])
        bias = sb("bias", [P, 3])
        tmp2 = sb("tmp2", [HC, 2])
        temp4 = sb("temp4", [HC, 4])
        bnst = sb("bnst", [P, 3, NB * 6])
        mv = sb("mv", [P, 3, 2])
        msq = sb("msq", [P, 3])
        parts = sb("parts", [P, 3, 3, 2], BF16)
        res1 = sb("res1", [P, 3, 2])
        res2 = sb("res2", [P, 3, 2])
        gsum = sb("gsum", [P, 3, 2])
        gvar = sb("gvar", [P, 3])
        grs = sb("grs", [P, 3])
        rb = sb("rb", [P, 2, 3])
        e16 = sb("e16", [P, 2, 320], F16)
        q16 = sb("q16", [P, 2, 2, 256], F16)
        z16 = sb("z16", [P, 2, C], F16)
        tq = sb("tq", [P, 3, 2, C], F16)
        pf = sb("pf", [P, 3, 2 * C])
        ph = sb("ph", [P, 3, 2 * C], F16)
        pl = sb("pl", [P, 3, 2 * C], F16)
        n8 = sb("n8", [HC, 8])
        r8 = sb("r8", [HC, 8])
        rk = sb("rk", [HC, 4])
        dq = sb("dq", [HC, 4, HC])
        rq = sb("rq", [HC, 4, HC])
        lg = sb("lg", [HC, 4, HC])
        lz = sb("lz", [HC, 4, D])
        ez = sb("ez", [HC, 4, D])
        mx = sb("mx", [HC, 4])
        sm = sb("sm", [HC, 4])
        a16 = sb("a16", [HC, 2, 4, D], F16)
        ax = sb("ax", [HC, 2, 4, NH, D], F16)
        vh = sb("vh", [HC, 2, 2 * C], F16)
        vl = sb("vl", [HC, 2, 2 * C], F16)
        mh0 = sb("mh0", [P, 2, C], F16)
        ml0 = sb("ml0", [P, 2, C], F16)
        mh1 = sb("mh1", [P, 3, P], F16)
        ml1 = sb("ml1", [P, 3, P], F16)
        st = xn[:, :, :].rearrange("p a n -> p (a n)")
        st_grp = st[:, 0:6 * P]
        st_id = st[:, 768:896]
        st_wo = st[0:HC, 896:896 + 2 * C].rearrange("p (j c) -> p j c", j=2)

        g_ps = ctx.enter_context(nc.psum_tensor("g_ps", [P, 2, 512], F32))
        s_ps = ctx.enter_context(nc.psum_tensor("s_ps", [P, 2, 512], F32))
        t_ps = ctx.enter_context(nc.psum_tensor("t_ps", [P, 2, 1024], F16))
        o_ps = ctx.enter_context(nc.psum_tensor("o_ps", [P, 2, 512], F32))
        z_ps = s_ps[:, 1, 0:C].bitcast(F16)

        c_in = sem("c_in")
        set_v = sem("set_v")
        fills = sem("fills")
        wv_tr = sem("wv_tr")
        x_in = [[sem(f"x_in{t}_{m}") for m in (0, 1)] for t in range(3)]
        stored = [sem(f"stored{t}") for t in range(3)]
        bn_done = sem("bn_done")
        aggr = sem("aggr")
        stat = sem("stat")
        gn_mm = sem("gn_mm")
        gstep = sem("gstep")
        norm = sem("norm")
        h_ok = sem("h_ok")
        xn_ok = sem("xn_ok")
        l_ok = sem("l_ok")
        tr_mm = sem("tr_mm")
        tok_a = sem("tok_a")
        tok_v = sem("tok_v")
        gram_mm = sem("gram_mm")
        e_ok = sem("e_ok")
        gfull = sem("gfull")
        gh_ok = sem("gh_ok")
        gl_ok = sem("gl_ok")
        z_mm = sem("z_mm")
        z_ok = sem("z_ok")
        t_mm = sem("t_mm")
        th_ok = sem("th_ok")
        tl_ok = sem("tl_ok")
        pf_ok = sem("pf_ok")
        ph_ok = sem("ph_ok")
        pl_ok = sem("pl_ok")
        nrm_mm = sem("nrm_mm")
        s_mm = sem("s_mm")
        n8_ok = sem("n8_ok")
        r8_ok = sem("r8_ok")
        dq_ok = sem("dq_ok")
        rk_ok = sem("rk_ok")
        rq_mm = sem("rq_mm")
        rq_ok = sem("rq_ok")
        var_ok = sem("var_ok")
        grs_ok = sem("grs_ok")
        soft = sem("soft")
        exp_ok = sem("exp_ok")
        attn_s = sem("attn_s")
        attn = sem("attn")
        v_mm = sem("v_mm")
        vh_ok = sem("vh_ok")
        vl_ok = sem("vl_ok")
        m_mm = sem("m_mm")
        mh_ok = sem("mh_ok")
        ml_ok = sem("ml_ok")
        out_mm = sem("out_mm")
        out_ok = sem("out_ok")
        STAT, GVAR, NORM, SOFT, ATTN = 6, 4, 2, 5, 5

        def need(eng, s, value):
            if not isinstance(value, int) or value > 0:
                eng.wait_ge(s, value)

        class Chain:

            def __init__(self, eng, s, base, length):
                self.eng, self.s, self.base, self.length, self.n = eng, s, base, length, 0

            def then(self, ins):
                ins.then_inc(self.s, 1)
                self.n += 1
                assert self.n <= self.length
                if self.n < self.length:
                    self.eng.wait_ge(self.s, self.base + self.n)

        def xcol(q, t, c, n):
            return x_sb[:, bass.ds((q % NX) * TILE + t * N + c, n)]

        def for_pairs(eng, step):
            step(-1)
            with eng.Fori(0, PAIRS // 2 - 1, 1) as i:
                for off in (0, 1):
                    step(2 * i + off, off, i)
            step(PAIRS - 2)
            step(PAIRS - 1)

        block = ctx.enter_context(nc.Block())

        @block.sync
        def _(sp):
            def fixed(v):
                return v if isinstance(v, int) else sp.snap(v)

            def ends(q):
                at, image = [fixed((q % NX) * TILE + t * N) for t in range(3)], [fixed(2 * q + b) for b in (0, 1)]
                def tile(dram, t):
                    rows = [(slice(0, P), slice(0, P), t // 2)] if t != 1 else \
                        [(slice(C1 * b, C1 * b + C1), slice(P, C), b) for b in (0, 1)]
                    return [(x_sb[part, bass.ds(at[t], N)],
                             dram[bass.ds(image[b], 1), chan, :].rearrange("o c n -> (o c) n")) for part, chan, b in rows]
                return tile

            def load(tile, par, t):
                for chip, dram in tile(x_d, t):
                    sp.dma_start(chip, dram).then_inc(x_in[t][par], 16)

            def store(tile, t):
                for chip, dram in tile(o_d, t):
                    sp.dma_start(dram, chip).then_inc(stored[t], 16)

            def step(p, par, more):
                out_tile, done = ends(p), {t: fixed(p * NO + (k + 1) * NB) for k, t in enumerate((0, 2, 1))}
                in_tile, landed = ends(p + NX), {t: fixed((p + 1) * (32 if t == 1 else 16)) for t in range(3)}
                for t_out, t_in in ((0, None), (2, 0), (1, 2), (None, 1)):
                    if t_out is not None:
                        sp.wait_ge(out_ok, done[t_out])
                        store(out_tile, t_out)
                    if t_in is not None and more:
                        sp.wait_ge(stored[t_in], landed[t_in])
                        load(in_tile, 1 - par, t_in)

            for q in range(NX):
                if q == 2:
                    sp.wait_ge(bn_done, 3)
                for t in (0, 2, 1):
                    load(ends(q), q % 2, t)
            with sp.Fori(0, (PAIRS - NX) // 2, 1) as i:
                for off in (0, 1):
                    step(2 * i + off, off, True)
            for p in range((PAIRS - NX) // 2 * 2, PAIRS):
                step(p, p % 2, p + NX < PAIRS)
            for t in range(3):
                sp.wait_ge(stored[t], PAIRS * (32 if t == 1 else 16))

        @block.gpsimd
        def _(pool):
            def split(q, par, cs):
                for c in cs:
                    t, hf = CHUNKS[c]
                    pool.wait_ge(h_ok, q * NC_ + c + 1)
                    pool.wait_ge(xn_ok, q * NC_ + c + 1)
                    if c == 0:
                        need(pool, out_mm, (q - 1) * NO)
                    nc.gpsimd.tensor_tensor(l_sb[:, par, t, hf * HALF:hf * HALF + HALF], xn[:, c % 2, :],
                                            h_sb[:, par, t, hf * HALF:hf * HALF + HALF], ALU.subtract).then_inc(l_ok, 1)

            def group_power(q):
                pool.wait_ge(var_ok, q + 1)
                nc.gpsimd.tensor_tensor(grs[:, :], gvar[:, :], minus_half[:, :].to_broadcast([P, 3]), ALU.pow
                                        ).then_inc(grs_ok, 1)

            def norm_power(q):
                pool.wait_ge(n8_ok, q + 1)
                nc.gpsimd.tensor_tensor(r8[:, :], n8[:, :], minus_half[0:HC, :].to_broadcast([HC, 8]), ALU.pow
                                        ).then_inc(r8_ok, 1)

            def low_products(q):
                for k in range(3):
                    pool.wait_ge(ph_ok, 3 * q + k + 1)
                    nc.gpsimd.tensor_tensor(pl[:, k, :], pf[:, k, :], ph[:, k, :], ALU.subtract).then_inc(pl_ok, 1)

            def step(p, par=None, half=None):
                first = isinstance(p, int) and p < 0
                par = p % 2 if isinstance(p, int) else par
                if first:
                    group_power(0)
                    split(0, 0, range(NC_))
                more, norm_next = (not isinstance(p, int) or p + k < PAIRS for k in (1, 2))
                if norm_next:
                    group_power(p + 2)
                if more:
                    low_products(p + 1)
                if norm_next:
                    split(p + 2, par, range(2))
                if more:
                    norm_power(p + 1)
                if norm_next:
                    split(p + 2, par, range(2, NC_))

            pool.wait_ge(fills, 1)
            for_pairs(pool, step)

        @block.scalar
        def _(act):
            act.dma_start(st_grp, groups).then_inc(c_in, 16)
            act.dma_start(st_id, ident).then_inc(c_in, 16)
            act.dma_start(w0[:, :], w_qkv[0:P, :]).then_inc(c_in, 16)
            act.dma_start(w1[0:C1, :], w_qkv[P:C, :]).then_inc(c_in, 16)
            act.dma_start(w1[C1:P, :], w_qkv[P:C, :]).then_inc(c_in, 16)
            act.dma_start(mask[:, :], headmask).then_inc(c_in, 16)
            act.dma_start(st_wo, w_out.rearrange("(j p) c -> p j c", j=2)).then_inc(c_in, 16)
            with nc.allow_non_contiguous_dma(reason="biases and temperatures, once"):
                act.dma_start(bias[:, 0:1], b_out[0:P].rearrange("(p o) -> p o", o=1)).then_inc(c_in, 16)
                act.dma_start(bias[0:C1, 1:2], b_out[P:C].rearrange("(p o) -> p o", o=1)).then_inc(c_in, 16)
                act.dma_start(bias[C1:P, 1:2], b_out[P:C].rearrange("(p o) -> p o", o=1)).then_inc(c_in, 16)
                t_d = temperature.rearrange("a (j g) b c -> (a b c g) j", j=2)
                for g in range(NH):
                    act.dma_start(tmp2[g * D:g * D + D, :], t_d[g:g + 1, :].to_broadcast([D, 2])).then_inc(c_in, 16)

            def split(q, par, cs):
                for c in cs:
                    t, hf = CHUNKS[c]
                    if c == 0:
                        act.wait_ge(norm, (q + 1) * NORM)
                        need(act, out_mm, (q - 1) * NO)
                        if isinstance(q, int) and q == 0:
                            act.wait_ge(set_v, 2)
                    need(act, l_ok, q * NC_ + c - 1)
                    src = xcol(q, t, hf * HALF, HALF)
                    nc.scalar.activation(xn[:, c % 2, :], src, ACT.Identity,
                                         bias=rb[:, 1, t:t + 1], scale=rb[:, 0, t:t + 1]).then_inc(xn_ok, 1)
                    nc.scalar.activation(h_sb[:, par, t, hf * HALF:hf * HALF + HALF], src, ACT.Identity,
                                         bias=rb[:, 1, t:t + 1], scale=rb[:, 0, t:t + 1]).then_inc(h_ok, 1)

            def to_tok(q, j):
                act.wait_ge(tr_mm, q * SLOTS + j + 1)
                need(act, gram_mm, q * SLOTS + j + 1 - TOK_RING)
                nc.scalar.copy(tok[:, j % TOK_RING, :, :].rearrange("p b n -> p (b n)"), t_ps[:, j % 2, 0:768]
                               ).then_inc(tok_a, 1)

            def spread_norms(q):
                act.wait_ge(rq_mm, q + 1)
                nc.scalar.copy(rq[:, :, :].rearrange("p a c -> p (a c)"), s_ps[0:HC, 0, 0:4 * HC]).then_inc(rq_ok, 1)

            def exp(q):
                act.wait_ge(soft, (q + 1) * SOFT)
                nc.scalar.activation(ez[:, :, :], lz[:, :, :], ACT.Exp).then_inc(exp_ok, 1)

            def high_v(q):
                for b in (0, 1):
                    act.wait_ge(v_mm, 2 * q + b + 1)
                    nc.scalar.copy(vh[:, b, :], s_ps[0:HC, b, 0:2 * C]).then_inc(vh_ok, 1)

            def high_m(q):
                act.wait_ge(fills, 1)
                act.wait_ge(m_mm, 2 * q + 1)
                nc.scalar.mul(mh0[:, :, :].rearrange("p b c -> p (b c)"), s_ps[:, 0, 0:2 * C], M_EVAC).then_inc(mh_ok, 1)
                act.wait_ge(m_mm, 2 * q + 2)
                m1 = mh1[:, :, :].rearrange("p t c -> p (t c)")
                nc.scalar.mul(m1[0:C1, 0:C], s_ps[0:C1, 1, 0:C], M_EVAC)
                nc.scalar.mul(m1[C1:P, C:2 * C], s_ps[C1:P, 1, 0:C], M_EVAC).then_inc(mh_ok, 1)

            def small_gram(q):
                act.wait_ge(gram_mm, (q + 1) * SLOTS)
                for b in (0, 1):
                    nc.scalar.copy(e16[:, b, :], g_ps[:, b, G_C:512]).then_inc(e_ok, 1)

            def high_gram(q):
                for b in (0, 1):
                    act.wait_ge(gfull, 2 * q + b + 1)
                    nc.scalar.copy(q16[:, b, 0, :], g_ps[:, b, 0:256]).then_inc(gh_ok, 1)

            def high_t(q, k):
                src = g_ps[:, k, :] if k < 2 else s_ps[:, 0, :]
                act.wait_ge(t_mm, 3 * q + k + 1)
                nc.scalar.copy(tq[:, k, 0, :], src[:, 0:C]).then_inc(th_ok, 1)

            def high_p(q, k):
                act.wait_ge(pf_ok, 3 * q + k + 1)
                nc.scalar.copy(ph[:, k, :], pf[:, k, :]).then_inc(ph_ok, 1)

            LATE = 2

            def step(p, par=None, half=None):
                first = isinstance(p, int) and p < 0
                loop = not isinstance(p, int)
                par = p % 2 if not loop else par
                if first:
                    split(0, 0, range(NC_))
                gram, small = loop or p + 1 < PAIRS, not first
                late = {1: NC_ - 2, 4: NC_ - 1}
                for j in range(SLOTS):
                    if gram and not slot_is_vector(j):
                        to_tok(p + 1, j)
                    if gram and not first and j in late:
                        split(p + 1, 1 - par, [late[j]])
                    if small and j == 1:
                        spread_norms(p)
                    if small and j == 5:
                        exp(p)
                    if small and j == 10:
                        high_v(p)
                    if small and j == 13:
                        high_m(p)
                if gram:
                    small_gram(p + 1)
                    high_gram(p + 1)
                    high_t(p + 1, 0)
                    for k in (1, 2):
                        high_t(p + 1, k)
                        high_p(p + 1, k - 1)
                    high_p(p + 1, 2)
                if loop or p + 2 < PAIRS:
                    split(p + 2, par, range(NC_ - LATE))

            for_pairs(act, step)

        @block.vector
        def _(dve):
            V = nc.vector
            V.memset(minus_half[:, :], -0.5)
            V.memset(ones[:, 0:1], 1.0)
            V.memset(ones[0:C1, 1:2], 1.0)
            V.memset(ones[C1:P, 1:2], 0.0)
            V.memset(ones[0:C1, 2:3], 0.0)
            V.memset(ones[C1:P, 2:3], 1.0)
            V.memset(wl1[C1:P, :], 0.0)
            for z in (wkh1, wkl1):
                V.memset(z[C1:P, 0, :], 0.0)
                V.memset(z[0:C1, 1, :], 0.0)
            V.memset(mh1[:, :, :], 0.0)
            V.memset(ml1[:, :, :], 0.0).then_inc(fills, 1)
            dve.wait_ge(c_in, 16 * (10 + NH))
            V.tensor_copy(grp[:, :, :].rearrange("p a m -> p (a m)"), st_grp)
            V.tensor_copy(id16[:, :], st_id)
            V.tensor_copy(id32[:, :], st_id[0:HC, 0:HC])
            V.tensor_copy(mask16[:, :], mask[:, :])
            V.tensor_scalar(temp4[:, 0:2], tmp2[:, :], LOGIT_FACTOR, None, ALU.mult)
            V.tensor_scalar(temp4[:, 2:4], tmp2[:, :], LOGIT_FACTOR, None, ALU.mult)
            V.tensor_copy(bias[:, 2:3], bias[:, 0:1])
            qk = slice(0, 2 * C)
            V.tensor_scalar(wh0[:, :], w0[:, qk], W_SCALE, None, ALU.mult)
            V.tensor_scalar(wh1[:, :], w1[:, qk], W_SCALE, None, ALU.mult)
            for b in (0, 1):
                V.tensor_scalar(wkh1[C1 * b:C1 * b + C1, b, :], w1[C1 * b:C1 * b + C1, C:2 * C], W_SCALE, None, ALU.mult)
            V.tensor_scalar(woh[:, :, 0:C], st_wo, W_SCALE, None, ALU.mult)
            V.tensor_scalar(woh[:, :, C:C + P], st_wo[:, :, 0:P], W_SCALE, None, ALU.mult).then_inc(set_v, 1)
            dve.wait_ge(set_v, 1)
            dve.wait_ge(fills, 1)

            def low(dst, src, hi):
                return V.scalar_tensor_tensor(out=dst, in0=src, scalar=W_SCALE, in1=hi, op0=ALU.mult, op1=ALU.subtract)

            low(wl0[:, :], w0[:, qk], wh0[:, :])
            low(wl1[0:C1, :], w1[0:C1, qk], wh1[0:C1, :])
            for b in (0, 1):
                r = slice(C1 * b, C1 * b + C1)
                low(wkl1[r, b, :], w1[r, C:2 * C], wkh1[r, b, :])
            low(wol[:, :, 0:C], st_wo, woh[:, :, 0:C])
            low(wol[:, :, C:C + P], st_wo[:, :, 0:P], woh[:, :, C:C + P]).then_inc(set_v, 1)
            dve.wait_ge(wv_tr, 1)
            wv_ps = s_ps[0:HC, 0, 0:2 * C].rearrange("p (j c) -> p j c", j=2)
            V.tensor_scalar(wvh[:, :, :], wv_ps, W_SCALE, None, ALU.mult).then_inc(set_v, 1)
            dve.wait_ge(set_v, 3)
            low(wvl[:, :, :], wv_ps, wvh[:, :, :]).then_inc(set_v, 1)

            def piece(q, par, half, k):
                t, (c, w) = (0, 2, 1)[k // NB], BLOCKS[k % NB]
                if k % NB == 0:
                    dve.wait_ge(x_in[t][par], (half + 1) * (32 if t == 1 else 16))
                ins = V.bn_stats(bnst[:, t, 6 * (k % NB):6 * (k % NB) + 6], xcol(q, t, c, w))
                if k % NB == NB - 1:
                    ins.then_inc(bn_done, 1)

            def channel_stats(q):
                dve.wait_ge(bn_done, 3 * q + 3)
                V.memset(msq[:, :], 0.0)
                for t in range(3):
                    V.bn_aggr(mv[:, t, :], bnst[:, t, :]).then_inc(aggr, 1)
                dve.wait_ge(aggr, 3 * q + 3)
                ch = Chain(dve, stat, q * STAT, STAT)
                ch.then(V.tensor_tensor(msq[:, :], mv[:, :, 0], mv[:, :, 0], ALU.mult))
                ch.then(V.tensor_tensor(mv[:, :, 1], mv[:, :, 1], msq[:, :], ALU.add))
                ch.then(V.tensor_copy(parts[:, 0, :, :], mv[:, :, :]))
                ch.then(V.tensor_tensor(res1[:, :, :], mv[:, :, :], parts[:, 0, :, :], ALU.subtract))
                ch.then(V.tensor_copy(parts[:, 1, :, :], res1[:, :, :]))
                ch.then(V.tensor_tensor(parts[:, 2, :, :], res1[:, :, :], parts[:, 1, :, :], ALU.subtract))

            def group_variance(q):
                dve.wait_ge(gn_mm, q + 1)
                ch = Chain(dve, gstep, q * GVAR, GVAR)
                ch.then(V.tensor_reduce(gsum[:, :, :],
                                        s_ps[:, 1, GN_COL:GN_COL + 18].rearrange("p (t a s) -> p t s a", t=3, a=3),
                                        AX_X, ALU.add))
                ch.then(V.tensor_scalar(gsum[:, :, :], gsum[:, :, :], 1 / CG, None, ALU.mult))
                ch.then(V.tensor_tensor(gvar[:, :], gsum[:, :, 0], gsum[:, :, 0], ALU.mult))
                ch.then(V.tensor_tensor(gvar[:, :], gsum[:, :, 1], gvar[:, :], ALU.subtract))
                dve.wait_ge(gstep, (q + 1) * GVAR)
                V.tensor_scalar(gvar[:, :], gvar[:, :], GN_EPS, GN_EPS, ALU.add, ALU.max).then_inc(var_ok, 1)

            def scale_shift(q):
                dve.wait_ge(grs_ok, q + 1)
                need(dve, h_ok, q * NC_)
                ch = Chain(dve, norm, q * NORM, NORM)
                ch.then(V.tensor_scalar(rb[:, 0, :], grs[:, :], X_SCALE, None, ALU.mult))
                ch.then(V.scalar_tensor_tensor(out=rb[:, 1, :], in0=gsum[:, :, 0], scalar=-1.0, in1=rb[:, 0, :],
                                               op0=ALU.mult, op1=ALU.mult))

            def to_tok(q, j):
                dve.wait_ge(tr_mm, q * SLOTS + j + 1)
                need(dve, gram_mm, q * SLOTS + j + 1 - TOK_RING)
                V.tensor_copy(tok[:, j % TOK_RING, :, :].rearrange("p b n -> p (b n)"), t_ps[:, j % 2, 0:768]
                              ).then_inc(tok_v, 1)

            def norms(q):
                dve.wait_ge(nrm_mm, q + 1)
                V.tensor_scalar(n8[:, :], s_ps[0:HC, 0, 0:8], NORM_EPS ** 2 * NORM_FACTOR, None, ALU.max
                                ).then_inc(n8_ok, 1)

            def diagonals(q):
                dve.wait_ge(r8_ok, q + 1)
                V.tensor_tensor(dq[:, :, :], r8[:, 4:8].unsqueeze(2).to_broadcast([HC, 4, HC]),
                                id32[:, :].unsqueeze(1).to_broadcast([HC, 4, HC]), ALU.mult).then_inc(dq_ok, 1)
                V.tensor_tensor(rk[:, :], r8[:, 0:4], temp4[:, :], ALU.mult).then_inc(rk_ok, 1)

            def softmax_in(q):
                dve.wait_ge(rq_ok, q + 1)
                dve.wait_ge(s_mm, q + 1)
                dve.wait_ge(rk_ok, q + 1)
                ch = Chain(dve, soft, q * SOFT, SOFT)
                ch.then(V.tensor_tensor(lg[:, :, :].rearrange("p a c -> p (a c)"), s_ps[0:HC, 1, 0:4 * HC],
                                        rq[:, :, :].rearrange("p a c -> p (a c)"), ALU.mult))
                ch.then(V.tensor_reduce(lz[:, :, :], lg[:, :, :].rearrange("p a (g d) -> p a d g", g=NH), AX_X, ALU.add))
                ch.then(V.tensor_tensor(lz[:, :, :], lz[:, :, :], rk[:, :].unsqueeze(2).to_broadcast([HC, 4, D]), ALU.mult))
                ch.then(V.tensor_reduce(mx[:, :], lz[:, :, :], AX_X, ALU.max))
                ch.then(V.tensor_tensor(lz[:, :, :], lz[:, :, :], mx[:, :].unsqueeze(2).to_broadcast([HC, 4, D]),
                                        ALU.subtract))

            def softmax_out(q):
                dve.wait_ge(exp_ok, q + 1)
                ch = Chain(dve, attn, q * ATTN, ATTN)
                ch.then(V.tensor_reduce(sm[:, :], ez[:, :, :], AX_X, ALU.add))
                ch.then(V.reciprocal(sm[:, :], sm[:, :]))
                ch.then(V.scalar_tensor_tensor(out=lz[:, :, :], in0=ez[:, :, :], scalar=A_SCALE,
                                               in1=sm[:, :].unsqueeze(2).to_broadcast([HC, 4, D]),
                                               op0=ALU.mult, op1=ALU.mult))
                V.tensor_copy(a16[:, 0, :, :], lz[:, :, :]).then_inc(attn_s, 1)
                dve.wait_ge(attn_s, 2 * q + 1)
                V.tensor_tensor(a16[:, 1, :, :], lz[:, :, :], a16[:, 0, :, :], ALU.subtract).then_inc(attn_s, 1)
                dve.wait_ge(attn_s, 2 * q + 2)
                m4 = mask16[:, :].rearrange("p (g d) -> p g d", g=NH)
                for i in (0, 1):
                    for a in range(4):
                        ins = V.tensor_tensor(ax[:, i, a, :, :], a16[:, i, a, :].unsqueeze(1).to_broadcast([HC, NH, D]),
                                              m4, ALU.mult)
                    ch.then(ins)

            def low_v(q):
                for b in (0, 1):
                    dve.wait_ge(vh_ok, 2 * q + b + 1)
                    V.tensor_tensor(vl[:, b, :], s_ps[0:HC, b, 0:2 * C], vh[:, b, :], ALU.subtract).then_inc(vl_ok, 1)

            def low_m(q):
                def lowm(dst, src, hi):
                    return V.scalar_tensor_tensor(out=dst, in0=src, scalar=M_EVAC, in1=hi, op0=ALU.mult, op1=ALU.subtract)
                dve.wait_ge(mh_ok, 2 * q + 1)
                lowm(ml0[:, :, :].rearrange("p b c -> p (b c)"), s_ps[:, 0, 0:2 * C],
                     mh0[:, :, :].rearrange("p b c -> p (b c)")).then_inc(ml_ok, 1)
                dve.wait_ge(mh_ok, 2 * q + 2)
                h1, l1 = (m[:, :, :].rearrange("p t c -> p (t c)") for m in (mh1, ml1))
                lowm(l1[0:C1, 0:C], s_ps[0:C1, 1, 0:C], h1[0:C1, 0:C])
                lowm(l1[C1:P, C:2 * C], s_ps[C1:P, 1, 0:C], h1[C1:P, C:2 * C]).then_inc(ml_ok, 1)

            def low_gram(q):
                for b in (0, 1):
                    dve.wait_ge(gh_ok, 2 * q + b + 1)
                    V.tensor_tensor(q16[:, b, 1, :], g_ps[:, b, 0:256], q16[:, b, 0, :], ALU.subtract
                                    ).then_inc(gl_ok, 1)

            def z_copy(q):
                dve.wait_ge(z_mm, q + 1)
                V.tensor_copy(z16[:, :, :].rearrange("p b c -> p (b c)"), z_ps).then_inc(z_ok, 1)

            def low_t(q, k):
                src = g_ps[:, k, :] if k < 2 else s_ps[:, 0, :]
                dve.wait_ge(th_ok, 3 * q + k + 1)
                w = (w0 if k < 2 else w1)[:, qk]
                V.tensor_tensor(pf[:, k, :], src[:, 0:2 * C], w, ALU.mult).then_inc(pf_ok, 1)
                V.tensor_tensor(tq[:, k, 1, :], src[:, 0:C], tq[:, k, 0, :], ALU.subtract).then_inc(tl_ok, 1)

            def result(q, par, n):
                t, c, w = OUTS[n]
                dve.wait_ge(out_mm, q * NO + n + 1)
                xs = xcol(q, t, c, w)
                V.scalar_tensor_tensor(out=xs, in0=o_ps[:, (par + n) % 2, 0:w], scalar=bias[:, t:t + 1], in1=xs,
                                       op0=ALU.add, op1=ALU.add).then_inc(out_ok, 1)

            def step(p, par=None, half=None):
                first = isinstance(p, int) and p < 0
                loop = not isinstance(p, int)
                if not loop:
                    par, half = p % 2, p // 2
                if first:
                    for k in range(3 * NB):
                        piece(0, 0, 0, k)
                    channel_stats(0)
                    group_variance(0)
                    scale_shift(0)
                gram, small, norm_next = loop or p + 1 < PAIRS, not first, loop or p + 2 < PAIRS
                pieces = list(range(3 * NB)) if norm_next else []
                if small:
                    diagonals(p)
                for j in range(SLOTS):
                    if gram and slot_is_vector(j):
                        to_tok(p + 1, j)
                    if small and j == 2:
                        softmax_in(p)
                    if small and j == 5:
                        softmax_out(p)
                    if small and j == 11:
                        low_v(p)
                    if small and j == 14:
                        low_m(p)
                    if j >= 6 and pieces:
                        piece(p + 2, par, half + 1, pieces.pop(0))
                for n in range(NO):
                    if small:
                        result(p, par, n)
                    if gram and n == 1:
                        low_gram(p + 1)
                    if pieces:
                        piece(p + 2, par, half + 1, pieces.pop(0))
                    if gram and n == 3:
                        z_copy(p + 1)
                    if norm_next and n == 4:
                        channel_stats(p + 2)
                    if norm_next and n == 6:
                        group_variance(p + 2)
                    if norm_next and n == 7:
                        scale_shift(p + 2)
                    if gram and n == 10:
                        norms(p + 1)
                    if gram and n in (5, 7, 8):
                        low_t(p + 1, {5: 0, 7: 1, 8: 2}[n])

            for_pairs(dve, step)

        @block.tensor
        def _(pe):
            def mm(dst, lhs, rhs, start, stop=False):
                return nc.tensor.matmul(dst, lhs, rhs, start=start, stop=stop, skip_group_check=True)

            pe.wait_ge(c_in, 16 * (10 + NH))
            for j in (0, 1):
                cols = slice(2 * C + HC * j, 2 * C + HC * j + HC)
                nc.tensor.transpose(s_ps[0:HC, 0, C * j:C * j + P], w0[:, cols], st_id)
                last = nc.tensor.transpose(s_ps[0:HC, 0, C * j + P:C * j + C], w1[0:C1, cols], st_id[0:C1, 0:C1])
            last.then_inc(wv_tr, 1)

            def group_sums(q):
                pe.wait_ge(stat, (q + 1) * STAT)
                for dst, srcs in ((0, ((0, 0), (1, 4))), (1, ((1, 1), (0, 2), (2, 3))), (2, ((2, 0), (1, 5)))):
                    for k, (src, g) in enumerate(srcs):
                        last = mm(s_ps[:, 1, GN_COL + 6 * dst:GN_COL + 6 * dst + 6], grp[:, g, :],
                                  parts[:, :, src, :], k == 0, k == len(srcs) - 1)
                last.then_inc(gn_mm, 1)

            def transposes(q, par, j):
                if j < 2:
                    need(pe, tok_v, q * NV)
                    need(pe, tok_a, q * NA)
                elif slot_is_vector(j - 2):
                    pe.wait_ge(tok_v, q * NV + (j - 2) // 3 + 1)
                else:
                    pe.wait_ge(tok_a, q * NA + (j - 2) - (j - 1) // 3 + 1)
                if j == 0:
                    pe.wait_ge(h_ok, q * NC_ + 3)
                    pe.wait_ge(l_ok, q * NC_ + 3)
                if j * P == HALF:
                    pe.wait_ge(h_ok, q * NC_ + 6)
                    pe.wait_ge(l_ok, q * NC_ + 6)
                bank = t_ps[:, j % 2, 0:768].rearrange("p (b n) -> p b n", b=2)
                px = slice(P * j, P * j + P)
                for b in (0, 1):
                    nc.tensor.transpose(bank[:, b, 0:P], h_sb[:, par, 2 * b, px], id16[:, :])
                    nc.tensor.transpose(bank[:, b, 256:384], l_sb[:, par, 2 * b, px], id16[:, :])
                nc.tensor.transpose(bank[:, :, P:P + C1], h_sb[:, par, 1, px], id16[:, :])
                nc.tensor.transpose(bank[:, :, P + C1:P + 2 * C1], l_sb[:, par, 1, px], id16[:, :]).then_inc(tr_mm, 1)

            def gram(q, j):
                if slot_is_vector(j):
                    pe.wait_ge(tok_v, q * NV + j // 3 + 1)
                else:
                    pe.wait_ge(tok_a, q * NA + j - (j + 1) // 3 + 1)
                if j == 0:
                    need(pe, tl_ok, 3 * q)
                    need(pe, pf_ok, 3 * q)
                first, end = j == 0, j == SLOTS - 1
                for b in (0, 1):
                    s = tok[:, j % TOK_RING, b, :]
                    bank = g_ps[:, b, :]
                    mm(bank.rearrange("p (r c) -> p r c", r=2)[:, :, 0:C], s[:, 0:P], s[:, 0:384], first)
                    mm(bank[:, G_C:G_C + C1], s[:, P:256], s[:, P:C], False)
                    last = mm(bank[:, G_B:G_B + C1], s[:, 256:384], s[:, P:C], False)
                last.then_inc(gram_mm, 1)

            def finish_gram(q):
                for b in (0, 1):
                    pe.wait_ge(e_ok, 2 * q + b + 1)
                    bank, e = g_ps[:, b, :], e16[:, b, :]
                    mm(bank[:, 0:P], e[:, 128:256], id16[:, :], False)
                    mm(bank[:, 0:P], id16[:, :], e[:, 128:256], False)
                    mm(bank[:, P:C], id16[:, :], e[:, 64:128], False)
                    mm(bank[:, P:C], id16[:, :], e[:, 256:320], False)
                    mm(bank[0:C1, G_C:G_C + C1], e[C1:P, 0:C1], id16[C1:P, C1:P], False)
                    mm(bank[0:C1, G_C:G_C + C1], id16[C1:P, C1:P], e[C1:P, 0:C1], False, True).then_inc(gfull, 1)

            def gram_weights(q, ready):
                z = z16
                if not ready:
                    pe.wait_ge(gl_ok, 2 * q + 2)
                else:
                    pe.wait_ge(z_ok, q + 1)
                for b in (0, 1):
                    dst = g_ps[:, b, 0:2 * C]
                    hi, lo = (q16[:, b, i, 0:P] for i in (0, 1))
                    if not ready:
                        mm(dst, hi, wh0[:, :], True)
                        mm(dst, hi, wl0[:, :], False)
                        mm(dst, lo, wh0[:, :], False)
                    else:
                        mm(dst, z[:, b, 0:P], wh1[:, :], False)
                        mm(dst, z[:, b, 0:P], wl1[:, :], False, True).then_inc(t_mm, 1)
                if not ready:
                    need(pe, ml_ok, 2 * q)
                for k in (range(3, 5) if ready else range(3)):
                    for b in (0, 1):
                        dst = s_ps[C1 * b:C1 * b + C1, 0, 0:2 * C]
                        hi, lo = (q16[:, b, i, P:C] for i in (0, 1))
                        lhs, rhs = ((hi, wh0), (hi, wl0), (lo, wh0), (z[:, b, P:C], wh1), (z[:, b, P:C], wl1))[k]
                        last = mm(dst, lhs, rhs[:, :], k == 0, k == 4)
                if ready:
                    last.then_inc(t_mm, 1)
                    return
                for b in (0, 1):
                    for i in (0, 1):
                        rows = slice(C1 * i, C1 * i + C1)
                        nc.tensor.transpose(z_ps[rows, C * b:C * b + P], q16[:, b, i, P:C], id16[:, :])
                        last = nc.tensor.transpose(z_ps[rows, C * b + P:C * b + C], q16[0:C1, b, i, C:256],
                                                   id16[0:C1, 0:C1])
                last.then_inc(z_mm, 1)

            def norms_and_scores(q):
                pe.wait_ge(ph_ok, 3 * q + 3)
                pe.wait_ge(pl_ok, 3 * q + 3)
                pe.wait_ge(tl_ok, 3 * q + 3)
                for m in range(8):
                    b, j = m // 2 % 2, m % 2
                    cols = slice((C if m < 4 else 0) + HC * j, (C if m < 4 else 0) + HC * j + HC)
                    terms = [(ph[:, b, cols], 0), (pl[:, b, cols], 0), (ph[:, 2, cols], 1 + b), (pl[:, 2, cols], 1 + b)]
                    for k, (lhs, o) in enumerate(terms):
                        last = mm(s_ps[0:HC, 0, m:m + 1], lhs, ones[:, o:o + 1], k == 0, k == 3)
                last.then_inc(nrm_mm, 1)
                for b in (0, 1):
                    for j in (0, 1):
                        kc = slice(HC * j, HC * j + HC)
                        wk = slice(C + HC * j, C + HC * j + HC)
                        dst = s_ps[0:HC, 1, HC * (2 * b + j):HC * (2 * b + j) + HC]
                        terms = [(wh0[:, wk], tq[:, b, 0, kc]), (wh0[:, wk], tq[:, b, 1, kc]), (wl0[:, wk], tq[:, b, 0, kc]),
                                 (wkh1[:, b, kc], tq[:, 2, 0, kc]), (wkh1[:, b, kc], tq[:, 2, 1, kc]),
                                 (wkl1[:, b, kc], tq[:, 2, 0, kc])]
                        for k, (lhs, rhs) in enumerate(terms):
                            last = mm(dst, lhs, rhs, k == 0, k == 5)
                last.then_inc(s_mm, 1)

            def spread_norms(q):
                pe.wait_ge(dq_ok, q + 1)
                mm(s_ps[0:HC, 0, 0:4 * HC], mask[:, :], dq[:, :, :].rearrange("p a c -> p (a c)"), True, True
                   ).then_inc(rq_mm, 1)

            def attn_values(q):
                pe.wait_ge(attn, (q + 1) * ATTN)
                for b in (0, 1):
                    for j in (0, 1):
                        a_hi, a_lo = (ax[:, i, 2 * b + j, :, :].rearrange("p g d -> p (g d)") for i in (0, 1))
                        dst = s_ps[0:HC, b, C * j:C * j + C]
                        mm(dst, a_hi, wvh[:, j, :], True)
                        mm(dst, a_hi, wvl[:, j, :], False)
                        last = mm(dst, a_lo, wvh[:, j, :], False, True)
                    last.then_inc(v_mm, 1)

            def folded_weights(q):
                pe.wait_ge(vl_ok, 2 * q + 2)
                for b in (0, 1):
                    for j in (0, 1):
                        c0 = C * j
                        dst = s_ps[:, 0, C * b:C * b + C]
                        mm(dst, vh[:, b, c0:c0 + P], woh[:, j, 0:C], j == 0)
                        mm(dst, vh[:, b, c0:c0 + P], wol[:, j, 0:C], False)
                        last = mm(dst, vl[:, b, c0:c0 + P], woh[:, j, 0:C], False, j == 1)
                last.then_inc(m_mm, 1)
                for j in (0, 1):
                    for k in range(3):
                        for b in (0, 1):
                            v, wo = ((vh, woh), (vh, wol), (vl, woh))[k]
                            last = mm(s_ps[C1 * b:C1 * b + C1, 1, 0:C], v[:, b, C * j + P:C * j + C],
                                      wo[:, j, P * b:P * b + C], j == 0 and k == 0, j == 1 and k == 2)
                last.then_inc(m_mm, 1)

            def result(q, par, n):
                t, c, w = OUTS[n]
                if n == 0:
                    pe.wait_ge(ml_ok, 2 * q + 2)
                if n >= 2:
                    pe.wait_ge(out_ok, q * NO + n - 1)
                dst = o_ps[:, (par + n) % 2, 0:w]
                h, l = (a[:, par, :, c:c + w] for a in (h_sb, l_sb))
                if t != 1:
                    b = t // 2
                    mm(dst, mh0[:, b, 0:P], h[:, t, :], True)
                    mm(dst, mh0[:, b, 0:P], l[:, t, :], False)
                    mm(dst, mh1[:, t, :], h[:, 1, :], False)
                    mm(dst, mh1[:, t, :], l[:, 1, :], False)
                    mm(dst, ml0[:, b, 0:P], h[:, t, :], False)
                    mm(dst, ml1[:, t, :], h[:, 1, :], False, True).then_inc(out_mm, 1)
                else:
                    mm(dst, mh1[:, 1, :], h[:, 1, :], True)
                    mm(dst, mh1[:, 1, :], l[:, 1, :], False)
                    mm(dst, ml1[:, 1, :], h[:, 1, :], False)
                    for k, (m, a) in enumerate(((mh0, h), (mh0, l), (ml0, h))):
                        for b in (0, 1):
                            last = mm(dst[C1 * b:C1 * b + C1, :], m[:, b, P:C], a[:, 2 * b, :], False, k == 2)
                    last.then_inc(out_mm, 1)

            def step(p, par=None, half=None):
                first = isinstance(p, int) and p < 0
                loop = not isinstance(p, int)
                par = p % 2 if not loop else par
                if first:
                    pe.wait_ge(set_v, 4)
                    pe.wait_ge(fills, 1)
                    group_sums(0)
                more, small, norm_next = loop or p + 1 < PAIRS, not first, loop or p + 2 < PAIRS
                if more:
                    transposes(p + 1, 1 - par, 0)
                    transposes(p + 1, 1 - par, 1)
                for j in range(SLOTS):
                    if more:
                        gram(p + 1, j)
                        if j + 2 < SLOTS:
                            transposes(p + 1, 1 - par, j + 2)
                    if small and j == 0:
                        spread_norms(p)
                    if small and j == 8:
                        attn_values(p)
                    if small and j == 11:
                        folded_weights(p)
                for n in range(NO):
                    if small:
                        result(p, par, n)
                    if more and n == 0:
                        finish_gram(p + 1)
                    if more and n == 2:
                        gram_weights(p + 1, False)
                    if more and n == 4:
                        gram_weights(p + 1, True)
                    if norm_next and n == 5:
                        group_sums(p + 2)
                    if more and n == 9:
                        norms_and_scores(p + 1)

            for_pairs(pe, step)


def constants():
    C, C1 = 192, 64
    channel = [np.arange(P), P + np.arange(P) % C1, np.arange(P)]
    image = [np.zeros(P, int), np.arange(P) // C1, np.ones(P, int)]
    grp = np.zeros((P, 6, P), np.float32)
    for n, (src, dst) in enumerate(((0, 0), (1, 1), (0, 1), (2, 1), (1, 0), (1, 2))):
        grp[:, n, :] = ((channel[src] // CG)[:, None] == (channel[dst] // CG)[None]) & \
            (image[src][:, None] == image[dst][None])
    head = np.arange(C // 2) // (C // HEADS)
    return {"ident": np.eye(P, dtype=np.float32), "groups": grp.reshape(P, 6 * P),
            "headmask": (head[:, None] == head[None]).astype(np.float32)}


_INS = ['x', 'L0_conv_w_qkv', 'L0_conv_temperature', 'L0_conv_w_out', 'L0_conv_b_out']
_OUTS = [((16, 192, 48, 48), 'float32')]


def kernel(**inputs):
    import numpy as _np
    import concourse.bacc as _bacc
    from concourse import mybir as _mybir
    from concourse.bass_utils import run_bass_kernel_spmd as _run

    nc = _bacc.Bacc("TRN2", target_bir_lowering=False, num_devices=1)
    arrays, args = {}, []
    given = {name: _np.ascontiguousarray(inputs[name]) for name in _INS}
    given.update(constants())
    for name, a in given.items():
        arrays[f"in_{name}_dram"] = a
        args.append(nc.dram_tensor(f"in_{name}_dram", a.shape, _mybir.dt.from_np(a.dtype), kind="ExternalInput").ap())
    for i, (shape, dtype) in enumerate(_OUTS):
        dt = _mybir.dt.from_np(_np.dtype(dtype))
        args.append(nc.dram_tensor(f"out_{i}_dram", shape, dt, kind="ExternalOutput").ap())
    preact_attention(nc, *args)
    r = _run(nc, [arrays], core_ids=[0])
    got = tuple(r.results[0][f"out_{i}_dram"] for i in range(len(_OUTS)))
    return got[0]
```

```python
from contextlib import ExitStack

import numpy as np

import concourse.bass as bass
from concourse import mybir

ALU = mybir.AluOpType
ACT = mybir.ActivationFunctionType
F32 = mybir.dt.float32
F16 = mybir.dt.float16
BF16 = mybir.dt.bfloat16
AX_X = mybir.AxisListType.X

P = 128
HEADS = 8
CG = 6
GN_EPS = 1e-5
NORM_EPS = 1e-12
NX = 3
TOK_RING = 3
RING = 4
AHEAD = 3
XN_RING = 3
GN_COL = 400

X_SCALE = 1 / 8
M_SCALE = 8.0
W_SCALE = 16.0
A_SCALE = 16.0
NORM_FACTOR = W_SCALE * X_SCALE ** 2
LOGIT_FACTOR = NORM_FACTOR / (W_SCALE ** 2 * X_SCALE ** 2)
M_EVAC = M_SCALE / (W_SCALE ** 2 * A_SCALE)

G_C, G_HL, G_B = 192, 256, 448


PE_A = {0: ["spread"], 8: ["v"], 11: ["m"]}
PE_B = {2: ["gram"], 4: ["w0"], 6: ["w1"], 7: ["sums"], 13: ["norms"]}
ACT_A = {0: ["h6", "x8"], 2: ["spread"], 3: ["h7"], 5: ["h8", "exp"], 10: ["v"], 13: ["m"]}
ACT_B = ["t0", "t1", "p0", "t2", "p1", "p2", 0, 1, 2, 3, 4, 5, "x6", "x7"]
POOL_B = ["power", "p0", "p1", "p2", 0, 1, 2, 3, 4, 5, "norms", 6, 7, 8]
VEC_A = {2: ["diag"], 3: ["soft_in"], 5: ["soft_out"], 7: ["v"], 15: ["m"]}
VEC_B = {2: ["gram"], 4: ["z"], 5: ["stats", "t0"], 6: ["t1"], 8: ["t2"], 10: ["var"], 12: ["scale"], 15:
         ["norms"]}
FIRST_PE_A = {5: ["sums"]}
FIRST_PE_B = {0: ["gram", "w0"], 1: ["w1"], 8: ["norms"]}
FIRST_ACT_A = {"start": ["z0", "z1", "z2", "z3"], 0: ["z4"], 1: ["z5"], 2: ["z6"], 4: ["z7"], 6: ["z8"], 9: [0],
               12: [1]}
FIRST_ACT_B = ["t0", "t1", 2, "t2", "p0", "p1", "p2", 3, 4, 5, "x6", "x7"]
FIRST_POOL_B = ["power", 0, 1, 2, "p0", "p1", 3, "p2", "norms", 4, 5, 6, 7, 8]
FIRST_VEC_A = {10: ["stats", "var"], 11: ["scale"]}
FIRST_VEC_B = {0: ["gram", "z", "t0", "t1", "t2", "norms"]}
FIRST_BN_A = {0: 8, 3: 1, 6: 4, 7: 2}
FIRST_BN_B = {}
BN_A = {6: 3, 8: 1, 9: 1, 10: 2, 13: 1, 14: 1, 15: 1, 17: 1}
BN_B = {1: 2, 2: 1, 4: 1}


VECTOR_SLOTS = (1, 2, 3, 5, 14, 17)


def slot_is_vector(j):
    return j in VECTOR_SLOTS


def preact_attention(nc, x, w_qkv, temperature, w_out, b_out, ident, groups, headmask, out):
    B, C, H, W = x.shape
    N = H * W
    D = C // HEADS
    C1 = C - P
    PAIRS = B // 2
    SLOTS = N // P
    HC = C // 2
    NH = HEADS // 2
    GROUPS = 3
    GW = N // GROUPS
    BW = GW // 2
    TILE = 3 * N
    BN = [(c, min(512, N - c)) for c in range(0, N, 512)]
    NB = len(BN)
    OUTS = [(t, g * GW + k * BW) for g in range(GROUPS) for t in (0, 2, 1) for k in (0, 1)]
    NO = len(OUTS)
    NV = sum(slot_is_vector(j) for j in range(SLOTS))
    NA = SLOTS - NV
    CHUNKS = [(t, g) for g in range(GROUPS) for t in (0, 2, 1)]
    NC_ = len(CHUNKS)
    assert (SLOTS + NO) % RING == 0 and NO % RING == SLOTS % RING
    assert C == 192 and GW % P == 0 and SLOTS % 6 == 0 and PAIRS % 2 == 0

    x_d = x.rearrange("b c h w -> b c (h w)")
    o_d = out.rearrange("b c h w -> b c (h w)")

    with ExitStack() as ctx:
        def sb(name, shape, dt=F32):
            return ctx.enter_context(nc.sbuf_tensor(name, shape, dt))

        def sem(name):
            return ctx.enter_context(nc.semaphore(name))

        x_sb = sb("x_sb", [P, NX * TILE])
        h_sb = sb("h_sb", [P, 2, 3, N], F16)
        l_sb = sb("l_sb", [P, 2, 3, N], F16)
        xn = sb("xn", [P, XN_RING, GW])
        tok = sb("tok", [P, TOK_RING, 2, 384], F16)
        w0 = sb("w0", [P, 3 * C])
        w1 = sb("w1", [P, 3 * C])
        wh0 = sb("wh0", [P, 2 * C], F16)
        wl0 = sb("wl0", [P, 2 * C], F16)
        wh1 = sb("wh1", [P, 2 * C], F16)
        wl1 = sb("wl1", [P, 2 * C], F16)
        wkh1 = sb("wkh1", [P, 2, C], F16)
        wkl1 = sb("wkl1", [P, 2, C], F16)
        wvh = sb("wvh", [HC, 2, C], F16)
        wvl = sb("wvl", [HC, 2, C], F16)
        woh = sb("woh", [HC, 2, C + P], F16)
        wol = sb("wol", [HC, 2, C + P], F16)
        id16 = sb("id16", [P, P], F16)
        grp = sb("grp", [P, 6, P], BF16)
        mask = sb("mask", [HC, HC])
        mask16 = sb("mask16", [HC, HC], F16)
        id32 = sb("id32", [HC, HC])
        ones = sb("ones", [P, 3], F16)
        minus_half = sb("minus_half", [P, 1])
        bias = sb("bias", [P, 3])
        tmp2 = sb("tmp2", [HC, 2])
        temp4 = sb("temp4", [HC, 4])
        bnst = sb("bnst", [P, 3, NB * 6])
        mv = sb("mv", [P, 3, 2])
        msq = sb("msq", [P, 3])
        parts = sb("parts", [P, 3, 3, 2], BF16)
        res1 = sb("res1", [P, 3, 2])
        res2 = sb("res2", [P, 3, 2])
        gsum = sb("gsum", [P, 3, 2])
        gvar = sb("gvar", [P, 3])
        grs = sb("grs", [P, 3])
        rb = sb("rb", [P, 2, 2, 3])
        e16 = sb("e16", [P, 2, 320], F16)
        q16 = sb("q16", [P, 2, 2, 256], F16)
        z16 = sb("z16", [P, 2, C], F16)
        tq = sb("tq", [P, 3, 2, C], F16)
        pf = sb("pf", [P, 3, 2 * C])
        ph = sb("ph", [P, 3, 2 * C], F16)
        pl = sb("pl", [P, 3, 2 * C], F16)
        n8 = sb("n8", [HC, 8])
        r8 = sb("r8", [HC, 8])
        rk = sb("rk", [HC, 4])
        dq = sb("dq", [HC, 4, HC])
        rq = sb("rq", [HC, 4, HC])
        lg = sb("lg", [HC, 4, HC])
        lz = sb("lz", [HC, 4, D])
        ez = sb("ez", [HC, 4, D])
        mx = sb("mx", [HC, 4])
        sm = sb("sm", [HC, 4])
        a16 = sb("a16", [HC, 2, 4, D], F16)
        ax = sb("ax", [HC, 2, 4, NH, D], F16)
        vh = sb("vh", [HC, 2, 2 * C], F16)
        vl = sb("vl", [HC, 2, 2 * C], F16)
        mh0 = sb("mh0", [P, 2, C], F16)
        ml0 = sb("ml0", [P, 2, C], F16)
        mh1 = sb("mh1", [P, 3, P], F16)
        ml1 = sb("ml1", [P, 3, P], F16)
        st = h_sb[:, 1, :, :].rearrange("p t n -> p (t n)").bitcast(F32)
        st_grp = st[:, 0:6 * P]
        st_id = st[:, 768:896]
        st_wo = st[0:HC, 896:896 + 2 * C].rearrange("p (j c) -> p j c", j=2)

        g_ps = ctx.enter_context(nc.psum_tensor("g_ps", [P, 2, 512], F32))
        s_ps = ctx.enter_context(nc.psum_tensor("s_ps", [P, 2, 512], F32))
        u_ps = ctx.enter_context(nc.psum_tensor("u_ps", [P, RING, 512], F32))
        z_ps = s_ps[:, 1, 0:C].bitcast(F16)

        def slot_ps(j):
            return u_ps[:, j % RING, 0:384].bitcast(F16)

        def block_ps(n):
            return u_ps[:, (SLOTS + n) % RING, 0:BW]

        c_group = sem("c_group")
        c_in = sem("c_in")
        set_v = sem("set_v")
        fills = sem("fills")
        wv_tr = sem("wv_tr")
        x_in = [[sem(f"x_in{t}_{m}") for m in (0, 1)] for t in range(3)]
        stored = [sem(f"stored{t}") for t in range(3)]
        bn_done = sem("bn_done")
        aggr = sem("aggr")
        stat = sem("stat")
        gn_mm = sem("gn_mm")
        gstep = sem("gstep")
        norm = sem("norm")
        h_ok = sem("h_ok")
        xn_ok = sem("xn_ok")
        l_ok = sem("l_ok")
        tr_mm = sem("tr_mm")
        tok_a = sem("tok_a")
        tok_v = sem("tok_v")
        gram_mm = sem("gram_mm")
        e_ok = sem("e_ok")
        gfull = sem("gfull")
        gh_ok = sem("gh_ok")
        gl_ok = sem("gl_ok")
        z_mm = sem("z_mm")
        z_ok = sem("z_ok")
        t_mm = sem("t_mm")
        th_ok = sem("th_ok")
        tl_ok = sem("tl_ok")
        pf_ok = sem("pf_ok")
        ph_ok = sem("ph_ok")
        pl_ok = sem("pl_ok")
        nrm_mm = sem("nrm_mm")
        s_mm = sem("s_mm")
        n8_ok = sem("n8_ok")
        r8_ok = sem("r8_ok")
        dq_ok = sem("dq_ok")
        rk_ok = sem("rk_ok")
        rq_mm = sem("rq_mm")
        rq_ok = sem("rq_ok")
        var_ok = sem("var_ok")
        grs_ok = sem("grs_ok")
        soft = sem("soft")
        exp_ok = sem("exp_ok")
        attn_s = sem("attn_s")
        attn = sem("attn")
        v_mm = sem("v_mm")
        vh_ok = sem("vh_ok")
        vl_ok = sem("vl_ok")
        m_mm = sem("m_mm")
        mh_ok = sem("mh_ok")
        ml_ok = sem("ml_ok")
        out_mm = sem("out_mm")
        out_ok = sem("out_ok")
        STAT, GVAR, NORM, SOFT, ATTN = 6, 4, 2, 5, 5

        def need(eng, s, value):
            if not isinstance(value, int) or value > 0:
                eng.wait_ge(s, value)

        class Chain:

            def __init__(self, eng, s, base, length):
                self.eng, self.s, self.base, self.length, self.n = eng, s, base, length, 0

            def then(self, ins):
                ins.then_inc(self.s, 1)
                self.n += 1
                assert self.n <= self.length
                if self.n < self.length:
                    self.eng.wait_ge(self.s, self.base + self.n)

        def xcol(q, t, c, n):
            return x_sb[:, bass.ds((q % NX) * TILE + t * N + c, n)]

        def for_pairs(eng, step):
            step(-1)
            with eng.Fori(0, PAIRS // 2 - 1, 1) as i:
                for off in (0, 1):
                    step(2 * i + off, off, i)
            step(PAIRS - 2)
            step(PAIRS - 1)

        block = ctx.enter_context(nc.Block())

        @block.sync
        def _(sp):
            def fixed(v):
                return v if isinstance(v, int) else sp.snap(v)

            def places(q):
                return [[fixed((q % NX) * TILE + t * N + g * GW) for t in range(3)] for g in range(GROUPS)]

            def images(q):
                return [fixed(2 * q + b) for b in (0, 1)]

            def ends(at, image, dram, t, c, n):
                rows = [(slice(0, P), slice(0, P), t // 2)] if t != 1 else \
                    [(slice(C1 * b, C1 * b + C1), slice(P, C), b) for b in (0, 1)]
                return [(x_sb[part, bass.ds(at[t], n)],
                         dram[bass.ds(image[b], 1), chan, c:c + n].rearrange("o c n -> (o c) n")) for part, chan, b in rows]

            def load(at, image, par, t):
                for chip, dram in ends(at[0], image, x_d, t, 0, N):
                    sp.dma_start(chip, dram).then_inc(x_in[t][par], 16)

            def step(p, par, more):
                at, image, done = places(p), images(p), [fixed((p + 1) * NO + 2 * k + 2) for k in range(3 * GROUPS)]
                image_in = images(p + NX)
                landed = {t: fixed((p + 1) * GROUPS * (32 if t == 1 else 16)) for t in range(3)}
                for k, (t, g) in enumerate(CHUNKS):
                    sp.wait_ge(out_ok, done[k])
                    for chip, dram in ends(at[g], image, o_d, t, g * GW, GW):
                        sp.dma_start(dram, chip).then_inc(stored[t], 16)
                if more:
                    for t in (0, 2, 1):
                        sp.wait_ge(stored[t], landed[t])
                        load(at, image_in, 1 - par, t)

            for q in range(NX):
                if q == 1:
                    sp.wait_ge(c_group, 32)
                    sp.wait_ge(c_in, 16 * (8 + NH))
                if q == 2:
                    sp.wait_ge(bn_done, 3)
                for t in (0, 2, 1):
                    load(places(q), images(q), q % 2, t)
            with sp.Fori(0, (PAIRS - NX) // 2, 1) as i:
                for off in (0, 1):
                    step(2 * i + off, off, True)
            for p in range((PAIRS - NX) // 2 * 2, PAIRS):
                step(p, p % 2, p + NX < PAIRS)
            for t in range(3):
                sp.wait_ge(stored[t], PAIRS * GROUPS * (32 if t == 1 else 16))

        @block.gpsimd
        def _(pool):
            def split(q, par, cs):
                for c in cs:
                    t, g = CHUNKS[c]
                    cols = slice(g * GW, g * GW + GW)
                    pool.wait_ge(h_ok, q * NC_ + c + 1)
                    pool.wait_ge(xn_ok, q * NC_ + c + 1)
                    nc.gpsimd.tensor_tensor(l_sb[:, par, t, cols], xn[:, c % XN_RING, :], h_sb[:, par, t, cols],
                                            ALU.subtract).then_inc(l_ok, 1)

            def group_power(q):
                pool.wait_ge(var_ok, q + 1)
                nc.gpsimd.tensor_tensor(grs[:, :], gvar[:, :], minus_half[:, :].to_broadcast([P, 3]), ALU.pow
                                        ).then_inc(grs_ok, 1)

            def norm_power(q):
                pool.wait_ge(n8_ok, q + 1)
                nc.gpsimd.tensor_tensor(r8[:, :], n8[:, :], minus_half[0:HC, :].to_broadcast([HC, 8]), ALU.pow
                                        ).then_inc(r8_ok, 1)

            def low_product(q, k):
                pool.wait_ge(ph_ok, 3 * q + k + 1)
                nc.gpsimd.tensor_tensor(pl[:, k, :], pf[:, k, :], ph[:, k, :], ALU.subtract).then_inc(pl_ok, 1)

            def step(p, par=None, half=None):
                first = isinstance(p, int) and p < 0
                par = p % 2 if isinstance(p, int) else par
                if first:
                    group_power(0)
                    split(0, 0, range(NC_))
                more, norm_next = (not isinstance(p, int) or p + k < PAIRS for k in (1, 2))
                for what in (FIRST_POOL_B if first else POOL_B):
                    if isinstance(what, int):
                        if norm_next:
                            split(p + 2, par, [what])
                    elif what == "power":
                        if norm_next:
                            group_power(p + 2)
                    elif more:
                        norm_power(p + 1) if what == "norms" else low_product(p + 1, int(what[1]))

            pool.wait_ge(fills, 1)
            for_pairs(pool, step)

        @block.scalar
        def _(act):
            act.dma_start(st_grp, groups).then_inc(c_group, 16)
            act.dma_start(st_id, ident).then_inc(c_group, 16)
            act.dma_start(w0[:, :], w_qkv[0:P, :]).then_inc(c_in, 16)
            act.dma_start(w1[0:C1, :], w_qkv[P:C, :]).then_inc(c_in, 16)
            act.dma_start(w1[C1:P, :], w_qkv[P:C, :]).then_inc(c_in, 16)
            act.dma_start(mask[:, :], headmask).then_inc(c_in, 16)
            act.dma_start(st_wo, w_out.rearrange("(j p) c -> p j c", j=2)).then_inc(c_in, 16)
            with nc.allow_non_contiguous_dma(reason="biases and temperatures, once"):
                act.dma_start(bias[:, 0:1], b_out[0:P].rearrange("(p o) -> p o", o=1)).then_inc(c_in, 16)
                act.dma_start(bias[0:C1, 1:2], b_out[P:C].rearrange("(p o) -> p o", o=1)).then_inc(c_in, 16)
                act.dma_start(bias[C1:P, 1:2], b_out[P:C].rearrange("(p o) -> p o", o=1)).then_inc(c_in, 16)
                t_d = temperature.rearrange("a (j g) b c -> (a b c g) j", j=2)
                for g in range(NH):
                    act.dma_start(tmp2[g * D:g * D + D, :], t_d[g:g + 1, :].to_broadcast([D, 2])).then_inc(c_in, 16)

            def chunk_value(q, par, c):
                t, g = CHUNKS[c]
                if c == 0:
                    act.wait_ge(norm, (q + 1) * NORM)
                    if isinstance(q, int) and q == 1:
                        act.wait_ge(set_v, 5)
                need(act, l_ok, q * NC_ + c + 1 - XN_RING)
                nc.scalar.activation(xn[:, c % XN_RING, :], xcol(q, t, g * GW, GW), ACT.Identity,
                                     bias=rb[:, par, 1, t:t + 1], scale=rb[:, par, 0, t:t + 1]).then_inc(xn_ok, 1)

            def chunk_high(q, par, c):
                t, g = CHUNKS[c]
                nc.scalar.activation(h_sb[:, par, t, g * GW:g * GW + GW], xcol(q, t, g * GW, GW), ACT.Identity,
                                     bias=rb[:, par, 1, t:t + 1], scale=rb[:, par, 0, t:t + 1]).then_inc(h_ok, 1)

            def split(q, par, what):
                if isinstance(what, int) and CHUNKS[what][0] == 0 and what // 3 < GROUPS - 1:
                    need(act, out_mm, (q - 2) * NO + (what // 3 + 1) * NO // GROUPS)
                if not isinstance(what, str) or what[0] == "x":
                    chunk_value(q, par, int(str(what)[-1]))
                if not isinstance(what, str) or what[0] == "h":
                    chunk_high(q, par, int(str(what)[-1]))

            def to_tok(q, j):
                act.wait_ge(tr_mm, q * SLOTS + j + 1)
                need(act, gram_mm, q * SLOTS + j + 1 - TOK_RING)
                nc.scalar.copy(tok[:, j % TOK_RING, :, :].rearrange("p b n -> p (b n)"), slot_ps(j)
                               ).then_inc(tok_a, 1)

            def spread_norms(q):
                act.wait_ge(rq_mm, q + 1)
                nc.scalar.copy(rq[:, :, :].rearrange("p a c -> p (a c)"), s_ps[0:HC, 0, 0:4 * HC]).then_inc(rq_ok, 1)

            def exp(q):
                act.wait_ge(soft, (q + 1) * SOFT)
                nc.scalar.activation(ez[:, :, :], lz[:, :, :], ACT.Exp).then_inc(exp_ok, 1)

            def high_v(q):
                for b in (0, 1):
                    act.wait_ge(v_mm, 2 * q + b + 1)
                    nc.scalar.copy(vh[:, b, :], s_ps[0:HC, b, 0:2 * C]).then_inc(vh_ok, 1)

            def high_m(q):
                act.wait_ge(fills, 1)
                act.wait_ge(m_mm, 2 * q + 1)
                nc.scalar.mul(mh0[:, :, :].rearrange("p b c -> p (b c)"), s_ps[:, 0, 0:2 * C], M_EVAC).then_inc(mh_ok, 1)
                act.wait_ge(m_mm, 2 * q + 2)
                m1 = mh1[:, :, :].rearrange("p t c -> p (t c)")
                nc.scalar.mul(m1[0:C1, 0:C], s_ps[0:C1, 1, 0:C], M_EVAC)
                nc.scalar.mul(m1[C1:P, C:2 * C], s_ps[C1:P, 1, 0:C], M_EVAC).then_inc(mh_ok, 1)

            def small_gram(q):
                act.wait_ge(gram_mm, (q + 1) * SLOTS)
                for b in (0, 1):
                    nc.scalar.copy(e16[:, b, :], g_ps[:, b, G_C:512]).then_inc(e_ok, 1)

            def high_gram(q):
                for b in (0, 1):
                    act.wait_ge(gfull, 2 * q + b + 1)
                    nc.scalar.copy(q16[:, b, 0, :], g_ps[:, b, 0:256]).then_inc(gh_ok, 1)

            def high_t(q, k):
                src = g_ps[:, k, :] if k < 2 else s_ps[:, 0, :]
                act.wait_ge(t_mm, 3 * q + k + 1)
                nc.scalar.copy(tq[:, k, 0, :], src[:, 0:C]).then_inc(th_ok, 1)

            def high_p(q, k):
                act.wait_ge(pf_ok, 3 * q + k + 1)
                nc.scalar.copy(ph[:, k, :], pf[:, k, :]).then_inc(ph_ok, 1)

            small_steps = {"t0": lambda q: high_t(q, 0), "t1": lambda q: high_t(q, 1), "t2": lambda q: high_t(q, 2),
                           "p0": lambda q: high_p(q, 0), "p1": lambda q: high_p(q, 1), "p2": lambda q: high_p(q, 2),
                           "spread": spread_norms, "exp": exp, "v": high_v, "m": high_m}

            def of_chunk(what):
                return isinstance(what, int) or what[0] in "xh"

            def step(p, par=None, half=None):
                first = isinstance(p, int) and p < 0
                loop = not isinstance(p, int)
                par = p % 2 if not loop else par
                gram, small, norm_next = loop or p + 1 < PAIRS, not first, loop or p + 2 < PAIRS
                for j in (["start"] if first else []) + list(range(SLOTS)):
                    if j != "start" and gram and not slot_is_vector(j):
                        to_tok(p + 1, j)
                    for what in (FIRST_ACT_A if first else ACT_A).get(j, ()):
                        if first:
                            if str(what)[0] == "z":
                                split(0, 0, int(what[1:]))
                            else:
                                split(1, 1, what)
                        elif of_chunk(what):
                            if gram:
                                split(p + 1, 1 - par, what)
                        elif small:
                            small_steps[what](p)
                if gram:
                    small_gram(p + 1)
                    high_gram(p + 1)
                for what in (FIRST_ACT_B if first else ACT_B):
                    if of_chunk(what):
                        if norm_next:
                            split(p + 2, par, what)
                    elif gram:
                        small_steps[what](p + 1)

            for_pairs(act, step)

        @block.vector
        def _(dve):
            V = nc.vector
            V.memset(minus_half[:, :], -0.5).then_inc(out_ok, NO)
            V.memset(ones[:, 0:1], 1.0)
            V.memset(ones[0:C1, 1:2], 1.0)
            V.memset(ones[C1:P, 1:2], 0.0)
            V.memset(ones[0:C1, 2:3], 0.0)
            V.memset(ones[C1:P, 2:3], 1.0)
            V.memset(wl1[C1:P, :], 0.0)
            for z in (wkh1, wkl1):
                V.memset(z[C1:P, 0, :], 0.0)
                V.memset(z[0:C1, 1, :], 0.0)
            V.memset(mh1[:, :, :], 0.0)
            V.memset(ml1[:, :, :], 0.0).then_inc(fills, 1)
            qk = slice(0, 2 * C)

            def group_constants():
                dve.wait_ge(c_group, 32)
                V.tensor_copy(grp[:, :, :].rearrange("p a m -> p (a m)"), st_grp)
                V.tensor_copy(id16[:, :], st_id)
                V.tensor_copy(id32[:, :], st_id[0:HC, 0:HC]).then_inc(set_v, 1)

            def weight_constants():
                dve.wait_ge(c_in, 16 * (8 + NH))
                V.tensor_copy(mask16[:, :], mask[:, :])
                V.tensor_scalar(temp4[:, 0:2], tmp2[:, :], LOGIT_FACTOR, None, ALU.mult)
                V.tensor_scalar(temp4[:, 2:4], tmp2[:, :], LOGIT_FACTOR, None, ALU.mult)
                V.tensor_copy(bias[:, 2:3], bias[:, 0:1])
                V.tensor_scalar(wh0[:, :], w0[:, qk], W_SCALE, None, ALU.mult)
                V.tensor_scalar(wh1[:, :], w1[:, qk], W_SCALE, None, ALU.mult)
                for b in (0, 1):
                    V.tensor_scalar(wkh1[C1 * b:C1 * b + C1, b, :], w1[C1 * b:C1 * b + C1, C:2 * C], W_SCALE, None, ALU.mult)
                V.tensor_scalar(woh[:, :, 0:C], st_wo, W_SCALE, None, ALU.mult)
                V.tensor_scalar(woh[:, :, C:C + P], st_wo[:, :, 0:P], W_SCALE, None, ALU.mult).then_inc(set_v, 1)
                dve.wait_ge(set_v, 2)
                dve.wait_ge(fills, 1)

                def low(dst, src, hi):
                    return V.scalar_tensor_tensor(out=dst, in0=src, scalar=W_SCALE, in1=hi, op0=ALU.mult, op1=ALU.subtract)

                low(wl0[:, :], w0[:, qk], wh0[:, :])
                low(wl1[0:C1, :], w1[0:C1, qk], wh1[0:C1, :])
                for b in (0, 1):
                    r = slice(C1 * b, C1 * b + C1)
                    low(wkl1[r, b, :], w1[r, C:2 * C], wkh1[r, b, :])
                low(wol[:, :, 0:C], st_wo, woh[:, :, 0:C])
                low(wol[:, :, C:C + P], st_wo[:, :, 0:P], woh[:, :, C:C + P]).then_inc(set_v, 1)
                dve.wait_ge(wv_tr, 1)
                wv_ps = s_ps[0:HC, 0, 0:2 * C].rearrange("p (j c) -> p j c", j=2)
                V.tensor_scalar(wvh[:, :, :], wv_ps, W_SCALE, None, ALU.mult).then_inc(set_v, 1)
                dve.wait_ge(set_v, 4)
                low(wvl[:, :, :], wv_ps, wvh[:, :, :]).then_inc(set_v, 1)

            def piece(q, par, half, k):
                t, (c, w) = (0, 2, 1)[k // NB], BN[k % NB]
                if k % NB == 0:
                    dve.wait_ge(x_in[t][par], (half + 1) * (32 if t == 1 else 16))
                ins = V.bn_stats(bnst[:, t, 6 * (k % NB):6 * (k % NB) + 6], xcol(q, t, c, w))
                if k % NB == NB - 1:
                    ins.then_inc(bn_done, 1)

            def channel_stats(q):
                dve.wait_ge(bn_done, 3 * q + 3)
                V.memset(msq[:, :], 0.0)
                for t in range(3):
                    V.bn_aggr(mv[:, t, :], bnst[:, t, :]).then_inc(aggr, 1)
                dve.wait_ge(aggr, 3 * q + 3)
                ch = Chain(dve, stat, q * STAT, STAT)
                ch.then(V.tensor_tensor(msq[:, :], mv[:, :, 0], mv[:, :, 0], ALU.mult))
                ch.then(V.tensor_tensor(mv[:, :, 1], mv[:, :, 1], msq[:, :], ALU.add))
                ch.then(V.tensor_copy(parts[:, 0, :, :], mv[:, :, :]))
                ch.then(V.tensor_tensor(res1[:, :, :], mv[:, :, :], parts[:, 0, :, :], ALU.subtract))
                ch.then(V.tensor_copy(parts[:, 1, :, :], res1[:, :, :]))
                ch.then(V.tensor_tensor(parts[:, 2, :, :], res1[:, :, :], parts[:, 1, :, :], ALU.subtract))

            def group_variance(q):
                dve.wait_ge(gn_mm, q + 1)
                ch = Chain(dve, gstep, q * GVAR, GVAR)
                ch.then(V.tensor_reduce(gsum[:, :, :],
                                        s_ps[:, 1, GN_COL:GN_COL + 18].rearrange("p (t a s) -> p t s a", t=3, a=3),
                                        AX_X, ALU.add))
                ch.then(V.tensor_scalar(gsum[:, :, :], gsum[:, :, :], 1 / CG, None, ALU.mult))
                ch.then(V.tensor_tensor(gvar[:, :], gsum[:, :, 0], gsum[:, :, 0], ALU.mult))
                ch.then(V.tensor_tensor(gvar[:, :], gsum[:, :, 1], gvar[:, :], ALU.subtract))
                dve.wait_ge(gstep, (q + 1) * GVAR)
                V.tensor_scalar(gvar[:, :], gvar[:, :], GN_EPS, GN_EPS, ALU.add, ALU.max).then_inc(var_ok, 1)

            def scale_shift(q, par):
                dve.wait_ge(grs_ok, q + 1)
                need(dve, h_ok, (q - 1) * NC_)
                ch = Chain(dve, norm, q * NORM, NORM)
                ch.then(V.tensor_scalar(rb[:, par, 0, :], grs[:, :], X_SCALE, None, ALU.mult))
                ch.then(V.scalar_tensor_tensor(out=rb[:, par, 1, :], in0=gsum[:, :, 0], scalar=-1.0, in1=rb[:, par, 0, :],
                                               op0=ALU.mult, op1=ALU.mult))

            def to_tok(q, j):
                dve.wait_ge(tr_mm, q * SLOTS + j + 1)
                need(dve, gram_mm, q * SLOTS + j + 1 - TOK_RING)
                V.tensor_copy(tok[:, j % TOK_RING, :, :].rearrange("p b n -> p (b n)"), slot_ps(j)
                              ).then_inc(tok_v, 1)

            def norms(q):
                dve.wait_ge(nrm_mm, q + 1)
                V.tensor_scalar(n8[:, :], s_ps[0:HC, 0, 0:8], NORM_EPS ** 2 * NORM_FACTOR, None, ALU.max
                                ).then_inc(n8_ok, 1)

            def diagonals(q):
                dve.wait_ge(r8_ok, q + 1)
                V.tensor_tensor(dq[:, :, :], r8[:, 4:8].unsqueeze(2).to_broadcast([HC, 4, HC]),
                                id32[:, :].unsqueeze(1).to_broadcast([HC, 4, HC]), ALU.mult).then_inc(dq_ok, 1)
                V.tensor_tensor(rk[:, :], r8[:, 0:4], temp4[:, :], ALU.mult).then_inc(rk_ok, 1)

            def softmax_in(q):
                dve.wait_ge(rq_ok, q + 1)
                dve.wait_ge(s_mm, q + 1)
                dve.wait_ge(rk_ok, q + 1)
                ch = Chain(dve, soft, q * SOFT, SOFT)
                ch.then(V.tensor_tensor(lg[:, :, :].rearrange("p a c -> p (a c)"), s_ps[0:HC, 1, 0:4 * HC],
                                        rq[:, :, :].rearrange("p a c -> p (a c)"), ALU.mult))
                ch.then(V.tensor_reduce(lz[:, :, :], lg[:, :, :].rearrange("p a (g d) -> p a d g", g=NH), AX_X, ALU.add))
                ch.then(V.tensor_tensor(lz[:, :, :], lz[:, :, :], rk[:, :].unsqueeze(2).to_broadcast([HC, 4, D]), ALU.mult))
                ch.then(V.tensor_reduce(mx[:, :], lz[:, :, :], AX_X, ALU.max))
                ch.then(V.tensor_tensor(lz[:, :, :], lz[:, :, :], mx[:, :].unsqueeze(2).to_broadcast([HC, 4, D]),
                                        ALU.subtract))

            def softmax_out(q):
                dve.wait_ge(exp_ok, q + 1)
                ch = Chain(dve, attn, q * ATTN, ATTN)
                ch.then(V.tensor_reduce(sm[:, :], ez[:, :, :], AX_X, ALU.add))
                ch.then(V.reciprocal(sm[:, :], sm[:, :]))
                ch.then(V.scalar_tensor_tensor(out=lz[:, :, :], in0=ez[:, :, :], scalar=A_SCALE,
                                               in1=sm[:, :].unsqueeze(2).to_broadcast([HC, 4, D]),
                                               op0=ALU.mult, op1=ALU.mult))
                V.tensor_copy(a16[:, 0, :, :], lz[:, :, :]).then_inc(attn_s, 1)
                dve.wait_ge(attn_s, 2 * q + 1)
                V.tensor_tensor(a16[:, 1, :, :], lz[:, :, :], a16[:, 0, :, :], ALU.subtract).then_inc(attn_s, 1)
                dve.wait_ge(attn_s, 2 * q + 2)
                m4 = mask16[:, :].rearrange("p (g d) -> p g d", g=NH)
                for i in (0, 1):
                    for a in range(4):
                        ins = V.tensor_tensor(ax[:, i, a, :, :], a16[:, i, a, :].unsqueeze(1).to_broadcast([HC, NH, D]),
                                              m4, ALU.mult)
                    ch.then(ins)

            def low_v(q):
                for b in (0, 1):
                    dve.wait_ge(vh_ok, 2 * q + b + 1)
                    V.tensor_tensor(vl[:, b, :], s_ps[0:HC, b, 0:2 * C], vh[:, b, :], ALU.subtract).then_inc(vl_ok, 1)

            def low_m(q):
                def lowm(dst, src, hi):
                    return V.scalar_tensor_tensor(out=dst, in0=src, scalar=M_EVAC, in1=hi, op0=ALU.mult, op1=ALU.subtract)
                dve.wait_ge(mh_ok, 2 * q + 1)
                lowm(ml0[:, :, :].rearrange("p b c -> p (b c)"), s_ps[:, 0, 0:2 * C],
                     mh0[:, :, :].rearrange("p b c -> p (b c)")).then_inc(ml_ok, 1)
                dve.wait_ge(mh_ok, 2 * q + 2)
                h1, l1 = (m[:, :, :].rearrange("p t c -> p (t c)") for m in (mh1, ml1))
                lowm(l1[0:C1, 0:C], s_ps[0:C1, 1, 0:C], h1[0:C1, 0:C])
                lowm(l1[C1:P, C:2 * C], s_ps[C1:P, 1, 0:C], h1[C1:P, C:2 * C]).then_inc(ml_ok, 1)

            def low_gram(q):
                for b in (0, 1):
                    dve.wait_ge(gh_ok, 2 * q + b + 1)
                    V.tensor_tensor(q16[:, b, 1, :], g_ps[:, b, 0:256], q16[:, b, 0, :], ALU.subtract
                                    ).then_inc(gl_ok, 1)

            def z_copy(q):
                dve.wait_ge(z_mm, q + 1)
                V.tensor_copy(z16[:, :, :].rearrange("p b c -> p (b c)"), z_ps).then_inc(z_ok, 1)

            def low_t(q, k):
                src = g_ps[:, k, :] if k < 2 else s_ps[:, 0, :]
                dve.wait_ge(th_ok, 3 * q + k + 1)
                w = (w0 if k < 2 else w1)[:, qk]
                V.tensor_tensor(pf[:, k, :], src[:, 0:2 * C], w, ALU.mult).then_inc(pf_ok, 1)
                V.tensor_tensor(tq[:, k, 1, :], src[:, 0:C], tq[:, k, 0, :], ALU.subtract).then_inc(tl_ok, 1)

            def result(q, n):
                (t, c), w = OUTS[n], BW
                dve.wait_ge(out_mm, q * NO + n + 1)
                xs = xcol(q, t, c, w)
                V.scalar_tensor_tensor(out=xs, in0=block_ps(n), scalar=bias[:, t:t + 1], in1=xs,
                                       op0=ALU.add, op1=ALU.add).then_inc(out_ok, 1)

            small_steps = {"gram": low_gram, "z": z_copy, "t0": lambda q: low_t(q, 0), "t1": lambda q: low_t(q, 1),
                           "t2": lambda q: low_t(q, 2), "norms": norms, "diag": diagonals, "soft_in": softmax_in,
                           "soft_out": softmax_out, "v": low_v, "m": low_m}

            def step(p, par=None, half=None):
                first = isinstance(p, int) and p < 0
                loop = not isinstance(p, int)
                if not loop:
                    par, half = p % 2, p // 2
                if first:
                    for k in range(3 * NB):
                        piece(0, 0, 0, k)
                        if k == NB - 1:
                            group_constants()
                    channel_stats(0)
                    group_variance(0)
                    scale_shift(0, 0)
                    weight_constants()
                gram, small, norm_next = loop or p + 1 < PAIRS, not first, loop or p + 2 < PAIRS
                pieces = list(range(3 * NB)) if norm_next else []

                def partial(count):
                    for _ in range(count if pieces else 0):
                        piece(p + 2, par, half + 1, pieces.pop(0))

                def norm_step(what):
                    if what == "scale":
                        scale_shift(p + 2, par)
                    else:
                        {"stats": channel_stats, "var": group_variance}[what](p + 2)

                for j in range(SLOTS):
                    if gram and slot_is_vector(j):
                        to_tok(p + 1, j)
                    for what in (FIRST_VEC_A if first else VEC_A).get(j, ()):
                        if what in ("stats", "var", "scale"):
                            if norm_next:
                                norm_step(what)
                        elif small:
                            small_steps[what](p)
                    partial((FIRST_BN_A if first else BN_A).get(j, 0))
                for n in range(NO):
                    if small:
                        result(p, n)
                    for what in (FIRST_VEC_B if first else VEC_B).get(n, ()):
                        if what in ("stats", "var", "scale"):
                            if norm_next:
                                norm_step(what)
                        elif gram:
                            small_steps[what](p + 1)
                    partial((FIRST_BN_B if first else BN_B).get(n, 0))
                assert not pieces

            for_pairs(dve, step)

        @block.tensor
        def _(pe):
            def mm(dst, lhs, rhs, start, stop=False):
                return nc.tensor.matmul(dst, lhs, rhs, start=start, stop=stop, skip_group_check=True)

            def transpose_wv():
                pe.wait_ge(c_in, 16 * (8 + NH))
                for j in (0, 1):
                    cols = slice(2 * C + HC * j, 2 * C + HC * j + HC)
                    nc.tensor.transpose(s_ps[0:HC, 0, C * j:C * j + P], w0[:, cols], st_id)
                    last = nc.tensor.transpose(s_ps[0:HC, 0, C * j + P:C * j + C], w1[0:C1, cols], st_id[0:C1, 0:C1])
                last.then_inc(wv_tr, 1)

            def group_sums(q):
                pe.wait_ge(stat, (q + 1) * STAT)
                for dst, srcs in ((0, ((0, 0), (1, 4))), (1, ((1, 1), (0, 2), (2, 3))), (2, ((2, 0), (1, 5)))):
                    for k, (src, g) in enumerate(srcs):
                        last = mm(s_ps[:, 1, GN_COL + 6 * dst:GN_COL + 6 * dst + 6], grp[:, g, :],
                                  parts[:, :, src, :], k == 0, k == len(srcs) - 1)
                last.then_inc(gn_mm, 1)

            def in_tok(q, j):
                before = sum(slot_is_vector(k) for k in range(j))
                if slot_is_vector(j):
                    pe.wait_ge(tok_v, q * NV + before + 1)
                else:
                    pe.wait_ge(tok_a, q * NA + j - before + 1)

            def transposes(q, par, j):
                if j < RING:
                    need(pe, out_ok, (q - 1) * NO + NO - RING + j + 1)
                else:
                    in_tok(q, j - RING)
                if j * P % GW == 0:
                    pe.wait_ge(h_ok, q * NC_ + 3 * (j * P // GW) + 3)
                    pe.wait_ge(l_ok, q * NC_ + 3 * (j * P // GW) + 3)
                bank = slot_ps(j).rearrange("p (b n) -> p b n", b=2)
                px = slice(P * j, P * j + P)
                for b in (0, 1):
                    nc.tensor.transpose(bank[:, b, 0:P], h_sb[:, par, 2 * b, px], id16[:, :])
                    nc.tensor.transpose(bank[:, b, 256:384], l_sb[:, par, 2 * b, px], id16[:, :])
                nc.tensor.transpose(bank[:, :, P:P + C1], h_sb[:, par, 1, px], id16[:, :])
                nc.tensor.transpose(bank[:, :, P + C1:P + 2 * C1], l_sb[:, par, 1, px], id16[:, :]).then_inc(tr_mm, 1)

            def gram(q, j):
                in_tok(q, j)
                if j == 0:
                    need(pe, tl_ok, 3 * q)
                    need(pe, pf_ok, 3 * q)
                first, end = j == 0, j == SLOTS - 1
                for b in (0, 1):
                    s = tok[:, j % TOK_RING, b, :]
                    bank = g_ps[:, b, :]
                    mm(bank.rearrange("p (r c) -> p r c", r=2)[:, :, 0:C], s[:, 0:P], s[:, 0:384], first)
                    mm(bank[:, G_C:G_C + C1], s[:, P:256], s[:, P:C], False)
                    last = mm(bank[:, G_B:G_B + C1], s[:, 256:384], s[:, P:C], False)
                last.then_inc(gram_mm, 1)

            def finish_gram(q):
                for b in (0, 1):
                    pe.wait_ge(e_ok, 2 * q + b + 1)
                    bank, e = g_ps[:, b, :], e16[:, b, :]
                    mm(bank[:, 0:P], e[:, 128:256], id16[:, :], False)
                    mm(bank[:, 0:P], id16[:, :], e[:, 128:256], False)
                    mm(bank[:, P:C], id16[:, :], e[:, 64:128], False)
                    mm(bank[:, P:C], id16[:, :], e[:, 256:320], False)
                    mm(bank[0:C1, G_C:G_C + C1], e[C1:P, 0:C1], id16[C1:P, C1:P], False)
                    mm(bank[0:C1, G_C:G_C + C1], id16[C1:P, C1:P], e[C1:P, 0:C1], False, True).then_inc(gfull, 1)

            def gram_weights(q, ready):
                z = z16
                if not ready:
                    pe.wait_ge(gl_ok, 2 * q + 2)
                else:
                    pe.wait_ge(z_ok, q + 1)
                for b in (0, 1):
                    dst = g_ps[:, b, 0:2 * C]
                    hi, lo = (q16[:, b, i, 0:P] for i in (0, 1))
                    if not ready:
                        mm(dst, hi, wh0[:, :], True)
                        mm(dst, hi, wl0[:, :], False)
                        mm(dst, lo, wh0[:, :], False)
                    else:
                        mm(dst, z[:, b, 0:P], wh1[:, :], False)
                        mm(dst, z[:, b, 0:P], wl1[:, :], False, True).then_inc(t_mm, 1)
                if not ready:
                    need(pe, ml_ok, 2 * q)
                for k in (range(3, 5) if ready else range(3)):
                    for b in (0, 1):
                        dst = s_ps[C1 * b:C1 * b + C1, 0, 0:2 * C]
                        hi, lo = (q16[:, b, i, P:C] for i in (0, 1))
                        lhs, rhs = ((hi, wh0), (hi, wl0), (lo, wh0), (z[:, b, P:C], wh1), (z[:, b, P:C], wl1))[k]
                        last = mm(dst, lhs, rhs[:, :], k == 0, k == 4)
                if ready:
                    last.then_inc(t_mm, 1)
                    return
                for b in (0, 1):
                    for i in (0, 1):
                        rows = slice(C1 * i, C1 * i + C1)
                        nc.tensor.transpose(z_ps[rows, C * b:C * b + P], q16[:, b, i, P:C], id16[:, :])
                        last = nc.tensor.transpose(z_ps[rows, C * b + P:C * b + C], q16[0:C1, b, i, C:256],
                                                   id16[0:C1, 0:C1])
                last.then_inc(z_mm, 1)

            def norms_and_scores(q):
                pe.wait_ge(ph_ok, 3 * q + 3)
                pe.wait_ge(pl_ok, 3 * q + 3)
                pe.wait_ge(tl_ok, 3 * q + 3)
                for m in range(8):
                    b, j = m // 2 % 2, m % 2
                    cols = slice((C if m < 4 else 0) + HC * j, (C if m < 4 else 0) + HC * j + HC)
                    terms = [(ph[:, b, cols], 0), (pl[:, b, cols], 0), (ph[:, 2, cols], 1 + b), (pl[:, 2, cols], 1 + b)]
                    for k, (lhs, o) in enumerate(terms):
                        last = mm(s_ps[0:HC, 0, m:m + 1], lhs, ones[:, o:o + 1], k == 0, k == 3)
                last.then_inc(nrm_mm, 1)
                for b in (0, 1):
                    for j in (0, 1):
                        kc = slice(HC * j, HC * j + HC)
                        wk = slice(C + HC * j, C + HC * j + HC)
                        dst = s_ps[0:HC, 1, HC * (2 * b + j):HC * (2 * b + j) + HC]
                        terms = [(wh0[:, wk], tq[:, b, 0, kc]), (wh0[:, wk], tq[:, b, 1, kc]), (wl0[:, wk], tq[:, b, 0, kc]),
                                 (wkh1[:, b, kc], tq[:, 2, 0, kc]), (wkh1[:, b, kc], tq[:, 2, 1, kc]),
                                 (wkl1[:, b, kc], tq[:, 2, 0, kc])]
                        for k, (lhs, rhs) in enumerate(terms):
                            last = mm(dst, lhs, rhs, k == 0, k == 5)
                last.then_inc(s_mm, 1)

            def spread_norms(q):
                pe.wait_ge(dq_ok, q + 1)
                mm(s_ps[0:HC, 0, 0:4 * HC], mask[:, :], dq[:, :, :].rearrange("p a c -> p (a c)"), True, True
                   ).then_inc(rq_mm, 1)

            def attn_values(q):
                pe.wait_ge(attn, (q + 1) * ATTN)
                for b in (0, 1):
                    for j in (0, 1):
                        a_hi, a_lo = (ax[:, i, 2 * b + j, :, :].rearrange("p g d -> p (g d)") for i in (0, 1))
                        dst = s_ps[0:HC, b, C * j:C * j + C]
                        mm(dst, a_hi, wvh[:, j, :], True)
                        mm(dst, a_hi, wvl[:, j, :], False)
                        last = mm(dst, a_lo, wvh[:, j, :], False, True)
                    last.then_inc(v_mm, 1)

            def folded_weights(q):
                pe.wait_ge(vl_ok, 2 * q + 2)
                for b in (0, 1):
                    for j in (0, 1):
                        c0 = C * j
                        dst = s_ps[:, 0, C * b:C * b + C]
                        mm(dst, vh[:, b, c0:c0 + P], woh[:, j, 0:C], j == 0)
                        mm(dst, vh[:, b, c0:c0 + P], wol[:, j, 0:C], False)
                        last = mm(dst, vl[:, b, c0:c0 + P], woh[:, j, 0:C], False, j == 1)
                last.then_inc(m_mm, 1)
                for j in (0, 1):
                    for k in range(3):
                        for b in (0, 1):
                            v, wo = ((vh, woh), (vh, wol), (vl, woh))[k]
                            last = mm(s_ps[C1 * b:C1 * b + C1, 1, 0:C], v[:, b, C * j + P:C * j + C],
                                      wo[:, j, P * b:P * b + C], j == 0 and k == 0, j == 1 and k == 2)
                last.then_inc(m_mm, 1)

            def result(q, par, n):
                (t, c), w = OUTS[n], BW
                if n == 0:
                    pe.wait_ge(ml_ok, 2 * q + 2)
                if n >= RING:
                    pe.wait_ge(out_ok, (q + 1) * NO + n - RING + 1)
                elif isinstance(q, int) and q == PAIRS - 1:
                    pe.wait_ge(out_ok, q * NO + NO - RING + (n + SLOTS) % RING + 1)
                dst = block_ps(n)
                h, l = (a[:, par, :, c:c + w] for a in (h_sb, l_sb))
                if t != 1:
                    b = t // 2
                    mm(dst, mh0[:, b, 0:P], h[:, t, :], True)
                    mm(dst, mh0[:, b, 0:P], l[:, t, :], False)
                    mm(dst, mh1[:, t, :], h[:, 1, :], False)
                    mm(dst, mh1[:, t, :], l[:, 1, :], False)
                    mm(dst, ml0[:, b, 0:P], h[:, t, :], False)
                    mm(dst, ml1[:, t, :], h[:, 1, :], False, True).then_inc(out_mm, 1)
                else:
                    mm(dst, mh1[:, 1, :], h[:, 1, :], True)
                    mm(dst, mh1[:, 1, :], l[:, 1, :], False)
                    mm(dst, ml1[:, 1, :], h[:, 1, :], False)
                    for k, (m, a) in enumerate(((mh0, h), (mh0, l), (ml0, h))):
                        for b in (0, 1):
                            last = mm(dst[C1 * b:C1 * b + C1, :], m[:, b, P:C], a[:, 2 * b, :], False, k == 2)
                    last.then_inc(out_mm, 1)

            small_steps = {"gram": finish_gram, "w0": lambda q: gram_weights(q, False),
                           "w1": lambda q: gram_weights(q, True), "norms": norms_and_scores,
                           "spread": spread_norms, "v": attn_values, "m": folded_weights}

            def step(p, par=None, half=None):
                first = isinstance(p, int) and p < 0
                loop = not isinstance(p, int)
                par = p % 2 if not loop else par
                if first:
                    pe.wait_ge(set_v, 1)
                    group_sums(0)
                    transpose_wv()
                more, small, norm_next = loop or p + 1 < PAIRS, not first, loop or p + 2 < PAIRS
                if more:
                    for j in range(AHEAD):
                        transposes(p + 1, 1 - par, j)
                for j in range(SLOTS):
                    if more:
                        gram(p + 1, j)
                        if j + AHEAD < SLOTS:
                            transposes(p + 1, 1 - par, j + AHEAD)
                    for what in (FIRST_PE_A if first else PE_A).get(j, ()):
                        if what == "sums":
                            if norm_next:
                                group_sums(p + 2)
                        elif small:
                            small_steps[what](p)
                if first:
                    pe.wait_ge(set_v, 5)
                    pe.wait_ge(fills, 1)
                for n in range(NO):
                    if small:
                        result(p, par, n)
                    for what in (FIRST_PE_B if first else PE_B).get(n, ()):
                        if what == "sums":
                            if norm_next:
                                group_sums(p + 2)
                        elif more:
                            small_steps[what](p + 1)

            for_pairs(pe, step)


def constants():
    C, C1 = 192, 64
    channel = [np.arange(P), P + np.arange(P) % C1, np.arange(P)]
    image = [np.zeros(P, int), np.arange(P) // C1, np.ones(P, int)]
    grp = np.zeros((P, 6, P), np.float32)
    for n, (src, dst) in enumerate(((0, 0), (1, 1), (0, 1), (2, 1), (1, 0), (1, 2))):
        grp[:, n, :] = ((channel[src] // CG)[:, None] == (channel[dst] // CG)[None]) & \
            (image[src][:, None] == image[dst][None])
    head = np.arange(C // 2) // (C // HEADS)
    return {"ident": np.eye(P, dtype=np.float32), "groups": grp.reshape(P, 6 * P),
            "headmask": (head[:, None] == head[None]).astype(np.float32)}


_INS = ['x', 'L0_conv_w_qkv', 'L0_conv_temperature', 'L0_conv_w_out', 'L0_conv_b_out']
_OUTS = [((16, 192, 48, 48), 'float32')]


def kernel(**inputs):
    import numpy as _np
    import concourse.bacc as _bacc
    from concourse import mybir as _mybir
    from concourse.bass_utils import run_bass_kernel_spmd as _run

    nc = _bacc.Bacc("TRN2", target_bir_lowering=False, num_devices=1)
    arrays, args = {}, []
    given = {name: _np.ascontiguousarray(inputs[name]) for name in _INS}
    given.update(constants())
    for name, a in given.items():
        arrays[f"in_{name}_dram"] = a
        args.append(nc.dram_tensor(f"in_{name}_dram", a.shape, _mybir.dt.from_np(a.dtype), kind="ExternalInput").ap())
    for i, (shape, dtype) in enumerate(_OUTS):
        dt = _mybir.dt.from_np(_np.dtype(dtype))
        args.append(nc.dram_tensor(f"out_{i}_dram", shape, dt, kind="ExternalOutput").ap())
    preact_attention(nc, *args)
    r = _run(nc, [arrays], core_ids=[0])
    got = tuple(r.results[0][f"out_{i}_dram"] for i in range(len(_OUTS)))
    return got[0]
```

```python
from contextlib import ExitStack

import numpy as np

import concourse.bass as bass
from concourse import mybir

ALU = mybir.AluOpType
ACT = mybir.ActivationFunctionType
F32 = mybir.dt.float32
F16 = mybir.dt.float16
BF16 = mybir.dt.bfloat16
AX_X = mybir.AxisListType.X

P = 128
HEADS = 8
CG = 6
GN_EPS = 1e-5
NORM_EPS = 1e-12
NX = 3
TOK_RING = 4
RING = 4
LOAD_LAG = 2
AHEAD = 3
XN_RING = 3
GN_COL = 400

X_SCALE = 1 / 8
M_SCALE = 8.0
W_SCALE = 16.0
A_SCALE = 16.0
NORM_FACTOR = W_SCALE * X_SCALE ** 2
LOGIT_FACTOR = NORM_FACTOR / (W_SCALE ** 2 * X_SCALE ** 2)
M_EVAC = M_SCALE / (W_SCALE ** 2 * A_SCALE)

G_C, G_B = 192, 448

PE_A = {1: ["spread"], 8: ["v"], 13: ["m"]}
PE_B = {0: ["gram"], 4: ["w0", "sums"], 6: ["w1"], 13: ["scores"], 15: ["norms"]}
ACT_A = {0: ["h6"], 3: ["x7", "x8", "spread", "h7"], 5: ["exp"], 8: ["h8"], 10: ["v"], 15: ["m"]}
ACT_B = ["t0", "t1", "t2", "p0", "p1", 0, "p2", 1, 2, 3, 4, 5, "x6"]
POOL_B = ["power", "p0", "p1", "p2", 0, 1, 2, 3, 4, "norms", 5, 6, 7, 8]
VEC_A = {1: ["diag"], 3: ["soft_in"], 4: ["soft_out"], 12: ["v"], 17: ["m"]}
VEC_B = {0: ["gram", "stats"], 4: ["z", "var"], 6: ["t0", "t1", "scale", "t2"], 11: ["norms"]}
FIRST_PE_A = {16: ["sums"]}
FIRST_PE_B = {0: ["gram"], 2: ["w0"], 7: ["w1", "scores"], 14: ["norms"]}
FIRST_ACT_A = {"start": ["z0", "z1", "z2", "z3", "z4", "z5"], 1: ["z6", "z7"], 2: ["z8"]}
FIRST_ACT_B = [0, "t0", "t1", "t2", "p0", "p1", 1, "p2", 2, 3, 4, 5, "x6"]
FIRST_POOL_B = ["power", 0, "p0", "p1", "p2", 1, "norms", 2, 3, 4, 5, 6, 7, 8]
FIRST_VEC_A = {"start": ["z0", "z1", "z2", "high", "z3", "z4", "low", "bn"], 1: ["z5"], 2: ["z6"], 3: ["z7"],
               4: ["bn"] * 4 + ["z8"] + ["bn"] * 10, 13: ["stats"], 16: ["var"], 17: ["scale"]}
FIRST_VEC_B = {0: ["gram", "z", "t0", "t1"], 1: ["t2", "norms"]}
BN_A = {6: 1, 8: 3, 9: 1, 10: 1, 13: 2, 15: 2, 16: 1, 17: 4}
BN_B = {}
VECTOR_SLOTS = (1, 2, 3, 14, 16)
LAST_PE_A = {0: ["m"]}
LAST_PE_B = {2: ["gram"], 4: ["w0"], 6: ["w1"], 9: ["scores"], 10: ["norms"], 14: ["spread"], 15: ["v"]}
LAST_ACT_A = {0: ["m"]}
LAST_ACT_B = ["t0", "t1", "p0", "t2", "p1", "p2", "spread", "exp", "v"]
LAST_POOL_B = ["p0", "p1", "p2", "norms"]
LAST_VEC_A = {0: ["m"]}
LAST_VEC_B = {0: ["gram"], 4: ["z"], 6: ["t0", "t1"], 7: ["t2"], 8: ["norms"], 11: ["diag"],
              14: ["soft_in", "soft_out"], 15: ["v"]}
SUMS_AT = next(n for n, what in PE_B.items() if "sums" in what)


def slot_is_vector(j):
    return j in VECTOR_SLOTS


def preact_attention(nc, x, w_qkv, temperature, w_out, b_out, ident, groups, headmask, out):
    B, C, H, W = x.shape
    N = H * W
    D = C // HEADS
    C1 = C - P
    PAIRS = B // 2
    SLOTS = N // P
    HC = C // 2
    NH = HEADS // 2
    GROUPS = 3
    GW = N // GROUPS
    BW = GW // 2
    TILE = 3 * N
    BN = [(c, min(512, N - c)) for c in range(0, N, 512)]
    NB = len(BN)
    OUTS = [(t, g * GW + k * BW) for g in range(GROUPS) for t in (0, 2, 1) for k in (0, 1)]
    NO = len(OUTS)
    NV = sum(slot_is_vector(j) for j in range(SLOTS))
    NA = SLOTS - NV
    CHUNKS = [(t, g) for g in range(GROUPS) for t in (0, 2, 1)]
    NC_ = len(CHUNKS)
    assert (SLOTS + NO) % RING == 0 and NO % RING == SLOTS % RING
    assert C == 192 and GW % P == 0 and SLOTS % 6 == 0 and PAIRS % 2 == 0

    x_d = x.rearrange("b c h w -> b c (h w)")
    o_d = out.rearrange("b c h w -> b c (h w)")

    with ExitStack() as ctx:
        def sb(name, shape, dt=F32):
            return ctx.enter_context(nc.sbuf_tensor(name, shape, dt))

        def sem(name):
            return ctx.enter_context(nc.semaphore(name))

        x_sb = sb("x_sb", [P, NX * TILE])
        h_sb = sb("h_sb", [P, 2, 3, N], F16)
        l_sb = sb("l_sb", [P, 2, 3, N], F16)
        hl = sb("hl", [P, 2, N], F16)
        xn = sb("xn", [P, XN_RING, GW])
        tok = sb("tok", [P, TOK_RING, 2, 384], F16)
        w0 = sb("w0", [P, 3 * C])
        w1 = sb("w1", [P, 3 * C])
        wh0 = sb("wh0", [P, 2 * C], F16)
        wl0 = sb("wl0", [P, 2 * C], F16)
        wh1 = sb("wh1", [P, 2 * C], F16)
        wl1 = sb("wl1", [P, 2 * C], F16)
        wkh1 = sb("wkh1", [P, 2, C], F16)
        wkl1 = sb("wkl1", [P, 2, C], F16)
        wvh = sb("wvh", [HC, 2, C], F16)
        wvl = sb("wvl", [HC, 2, C], F16)
        woh = sb("woh", [HC, 2, C + P], F16)
        wol = sb("wol", [HC, 2, C + P], F16)
        id16 = sb("id16", [P, P], F16)
        grp = sb("grp", [P, 6, P], BF16)
        mask = sb("mask", [HC, HC])
        mask16 = sb("mask16", [HC, HC], F16)
        id32 = sb("id32", [HC, HC])
        ones = sb("ones", [P, 3], F16)
        minus_half = sb("minus_half", [P, 1])
        bias = sb("bias", [P, 3])
        tmp2 = sb("tmp2", [HC, 2])
        temp4 = sb("temp4", [HC, 4])
        bnst = sb("bnst", [P, 3, NB * 6])
        mv = sb("mv", [P, 3, 2])
        msq = sb("msq", [P, 3])
        parts = sb("parts", [P, 3, 3, 2], BF16)
        res1 = sb("res1", [P, 3, 2])
        res2 = sb("res2", [P, 3, 2])
        gsum = sb("gsum", [P, 3, 2])
        gvar = sb("gvar", [P, 3])
        grs = sb("grs", [P, 3])
        rb = sb("rb", [P, 2, 2, 3])
        e16 = sb("e16", [P, 2, 320], F16)
        q16 = sb("q16", [P, 2, 2, 256], F16)
        z16 = sb("z16", [P, 2, C], F16)
        tq = sb("tq", [P, 3, 2, C], F16)
        pf = sb("pf", [P, 3, 2 * C])
        ph = sb("ph", [P, 3, 2 * C], F16)
        pl = sb("pl", [P, 3, 2 * C], F16)
        n8 = sb("n8", [HC, 8])
        r8 = sb("r8", [HC, 8])
        rk = sb("rk", [HC, 4])
        dq = sb("dq", [HC, 4, HC])
        rq = sb("rq", [HC, 4, HC])
        lg = sb("lg", [HC, 4, HC])
        lz = sb("lz", [HC, 4, D])
        ez = sb("ez", [HC, 4, D])
        mx = sb("mx", [HC, 4])
        sm = sb("sm", [HC, 4])
        a16 = sb("a16", [HC, 2, 4, D], F16)
        ax = sb("ax", [HC, 2, 4, NH, D], F16)
        vh = sb("vh", [HC, 2, 2 * C], F16)
        vl = sb("vl", [HC, 2, 2 * C], F16)
        mh0 = sb("mh0", [P, 2, C], F16)
        ml0 = sb("ml0", [P, 2, C], F16)
        mh1 = sb("mh1", [P, 2, C], F16)
        ml1 = sb("ml1", [P, 3, P], F16)
        st = h_sb[:, 1, :, :].rearrange("p t n -> p (t n)").bitcast(F32)
        st_grp = st[:, 0:6 * P]
        st_id = st[:, 768:896]
        st_wo = st[0:HC, 896:896 + 2 * C].rearrange("p (j c) -> p j c", j=2)

        g_ps = ctx.enter_context(nc.psum_tensor("g_ps", [P, 2, 512], F32))
        s_ps = ctx.enter_context(nc.psum_tensor("s_ps", [P, 2, 512], F32))
        u_ps = ctx.enter_context(nc.psum_tensor("u_ps", [P, RING, 512], F32))
        z_ps = s_ps[:, 1, 0:C].bitcast(F16)

        def slot_ps(j):
            return u_ps[:, j % RING, 0:384].bitcast(F16)

        def block_ps(n):
            return u_ps[:, (SLOTS + n) % RING, 0:BW]

        def sums_ps(first):
            return s_ps[:, 1, GN_COL:GN_COL + 18] if first else u_ps[:, (SLOTS + SUMS_AT + 3) % RING, GN_COL:GN_COL + 18]

        c_group = sem("c_group")
        c_in = sem("c_in")
        set_v = sem("set_v")
        fills = sem("fills")
        wv_tr = sem("wv_tr")
        x_in = [[sem(f"x_in{t}_{m}") for m in (0, 1)] for t in range(3)]
        stored = [sem(f"stored{t}") for t in range(3)]
        hl_in = [sem(f"hl_in{g}") for g in range(GROUPS)]
        bn_done = sem("bn_done")
        aggr = sem("aggr")
        stat = sem("stat")
        gn_mm = sem("gn_mm")
        gstep = sem("gstep")
        norm = sem("norm")
        h_ok = sem("h_ok")
        xn_ok = sem("xn_ok")
        xn0_ok = sem("xn0_ok")
        l_ok = sem("l_ok")
        tr_mm = sem("tr_mm")
        tok_a = sem("tok_a")
        tok_v = sem("tok_v")
        gram_mm = sem("gram_mm")
        e_ok = sem("e_ok")
        gfull = sem("gfull")
        gh_ok = sem("gh_ok")
        gl_ok = sem("gl_ok")
        z_mm = sem("z_mm")
        z_ok = sem("z_ok")
        t_mm = sem("t_mm")
        th_ok = sem("th_ok")
        tl_ok = sem("tl_ok")
        pf_ok = sem("pf_ok")
        ph_ok = sem("ph_ok")
        pl_ok = sem("pl_ok")
        nrm_mm = sem("nrm_mm")
        s_mm = sem("s_mm")
        n8_ok = sem("n8_ok")
        r8_ok = sem("r8_ok")
        dq_ok = sem("dq_ok")
        rk_ok = sem("rk_ok")
        rq_mm = sem("rq_mm")
        rq_ok = sem("rq_ok")
        var_ok = sem("var_ok")
        grs_ok = sem("grs_ok")
        soft = sem("soft")
        exp_ok = sem("exp_ok")
        attn_s = sem("attn_s")
        attn = sem("attn")
        v_mm = sem("v_mm")
        vh_ok = sem("vh_ok")
        vl_ok = sem("vl_ok")
        m_mm = sem("m_mm")
        mh_ok = sem("mh_ok")
        ml_ok = sem("ml_ok")
        out_mm = sem("out_mm")
        out_ok = sem("out_ok")
        STAT, GVAR, NORM, SOFT, ATTN = 6, 4, 2, 5, 5

        def need(eng, s, value):
            if not isinstance(value, int) or value > 0:
                eng.wait_ge(s, value)

        class Chain:

            def __init__(self, eng, s, base, length):
                self.eng, self.s, self.base, self.length, self.n = eng, s, base, length, 0

            def then(self, ins):
                ins.then_inc(self.s, 1)
                self.n += 1
                assert self.n <= self.length
                if self.n < self.length:
                    self.eng.wait_ge(self.s, self.base + self.n)

        def xcol(q, t, c, n):
            return x_sb[:, bass.ds((q % NX) * TILE + t * N + c, n)]

        def for_pairs(eng, step):
            step(-1)
            with eng.Fori(0, PAIRS // 2 - 1, 1) as i:
                for off in (0, 1):
                    step(2 * i + off, off, i)
            step(PAIRS - 2)
            step(PAIRS - 1)

        def hooks(p, first, usual, last, last_step):
            at_end = isinstance(p, int) and p == last_step
            return first if isinstance(p, int) and p < 0 else last if at_end else usual

        block = ctx.enter_context(nc.Block())

        @block.sync
        def _(sp):
            def fixed(v):
                return v if isinstance(v, int) else sp.snap(v)

            def places(q):
                return [[fixed((q % NX) * TILE + t * N + g * GW) for t in range(3)] for g in range(GROUPS)]

            def images(q):
                return [fixed(2 * q + b) for b in (0, 1)]

            def ends(at, image, dram, t, c, n):
                rows = [(slice(0, P), slice(0, P), t // 2)] if t != 1 else \
                    [(slice(C1 * b, C1 * b + C1), slice(P, C), b) for b in (0, 1)]
                return [(x_sb[part, bass.ds(at[t], n)],
                         dram[bass.ds(image[b], 1), chan, c:c + n].rearrange("o c n -> (o c) n")) for part, chan, b in rows]

            def load(at, image, par, t, g):
                for chip, dram in ends(at[g], image, x_d, t, g * GW, GW):
                    sp.dma_start(chip, dram).then_inc(x_in[t][par], 16)

            def copy_parts(par, g):
                cols = slice(g * GW, g * GW + GW)
                for b in (0, 1):
                    for i, part in enumerate((h_sb, l_sb)):
                        sp.dma_start(hl[C1 * i:C1 * i + C1, b, cols], part[C1 * b:C1 * b + C1, par, 1, cols]
                                     ).then_inc(hl_in[g], 16)

            def step(p, par, more):
                at, image, done = places(p), images(p), [fixed((p + 1) * NO + 2 * k + 2) for k in range(NC_)]
                image_in = images(p + NX)
                halves = [fixed((p + 1) * NC_ + 3 * g + 3) for g in range(GROUPS)]
                landed = [fixed((p * GROUPS + g + 1) * (32 if t == 1 else 16)) for t, g in CHUNKS]
                for k in range(NC_ + LOAD_LAG):
                    if k < NC_:
                        t, g = CHUNKS[k]
                        sp.wait_ge(out_ok, done[k])
                        for chip, dram in ends(at[g], image, o_d, t, g * GW, GW):
                            sp.dma_start(dram, chip).then_inc(stored[t], 16)
                        if t == 1 and not (isinstance(p, int) and p + 1 == PAIRS):
                            sp.wait_ge(l_ok, halves[g])
                            copy_parts(1 - par, g)
                    if more and k >= LOAD_LAG:
                        t, g = CHUNKS[k - LOAD_LAG]
                        sp.wait_ge(stored[t], landed[k - LOAD_LAG])
                        load(at, image_in, 1 - par, t, g)

            for q in range(NX):
                if q == 1:
                    sp.dma_start(w0[:, :], w_qkv[0:P, :]).then_inc(c_in, 16)
                    sp.dma_start(w1[0:C1, :], w_qkv[P:C, :]).then_inc(c_in, 16)
                    sp.dma_start(w1[C1:P, :], w_qkv[P:C, :]).then_inc(c_in, 16)
                    sp.dma_start(mask[:, :], headmask).then_inc(c_in, 16)
                    sp.dma_start(st_wo, w_out.rearrange("(j p) c -> p j c", j=2)).then_inc(c_in, 16)
                    with nc.allow_non_contiguous_dma(reason="biases and temperatures, once"):
                        sp.dma_start(bias[:, 0:1], b_out[0:P].rearrange("(p o) -> p o", o=1)).then_inc(c_in, 16)
                        sp.dma_start(bias[0:C1, 1:2], b_out[P:C].rearrange("(p o) -> p o", o=1)).then_inc(c_in, 16)
                        sp.dma_start(bias[C1:P, 1:2], b_out[P:C].rearrange("(p o) -> p o", o=1)).then_inc(c_in, 16)
                        t_d = temperature.rearrange("a (j g) b c -> (a b c g) j", j=2)
                        for g in range(NH):
                            sp.dma_start(tmp2[g * D:g * D + D, :], t_d[g:g + 1, :].to_broadcast([D, 2])).then_inc(c_in, 16)
                if q == 2:
                    sp.wait_ge(bn_done, 3)
                for t in (0, 2, 1):
                    for g in range(GROUPS):
                        load(places(q), images(q), q % 2, t, g)
            for g in range(GROUPS):
                sp.wait_ge(l_ok, 3 * g + 3)
                copy_parts(0, g)
            with sp.Fori(0, (PAIRS - NX) // 2, 1) as i:
                for off in (0, 1):
                    step(2 * i + off, off, True)
            for p in range((PAIRS - NX) // 2 * 2, PAIRS):
                step(p, p % 2, p + NX < PAIRS)
            for t in range(3):
                sp.wait_ge(stored[t], PAIRS * GROUPS * (32 if t == 1 else 16))

        @block.gpsimd
        def _(pool):
            def split(q, par, cs):
                for c in cs:
                    t, g = CHUNKS[c]
                    cols = slice(g * GW, g * GW + GW)
                    pool.wait_ge(h_ok, q * NC_ + c + 1)
                    if isinstance(q, int) and q == 0:
                        pool.wait_ge(xn0_ok, c + 1)
                    else:
                        pool.wait_ge(xn_ok, (q - 1) * NC_ + c + 1)
                    nc.gpsimd.tensor_tensor(l_sb[:, par, t, cols], xn[:, c % XN_RING, :], h_sb[:, par, t, cols],
                                            ALU.subtract).then_inc(l_ok, 1)

            def group_power(q):
                pool.wait_ge(var_ok, q + 1)
                nc.gpsimd.tensor_tensor(grs[:, :], gvar[:, :], minus_half[:, :].to_broadcast([P, 3]), ALU.pow
                                        ).then_inc(grs_ok, 1)

            def norm_power(q):
                pool.wait_ge(n8_ok, q + 1)
                nc.gpsimd.tensor_tensor(r8[:, :], n8[:, :], minus_half[0:HC, :].to_broadcast([HC, 8]), ALU.pow
                                        ).then_inc(r8_ok, 1)

            def low_product(q, k):
                pool.wait_ge(ph_ok, 3 * q + k + 1)
                nc.gpsimd.tensor_tensor(pl[:, k, :], pf[:, k, :], ph[:, k, :], ALU.subtract).then_inc(pl_ok, 1)

            def step(p, par=None, half=None):
                first = isinstance(p, int) and p < 0
                par = p % 2 if isinstance(p, int) else par
                if first:
                    group_power(0)
                    split(0, 0, range(NC_))
                more, norm_next = (not isinstance(p, int) or p + k < PAIRS for k in (1, 2))
                for what in hooks(p, FIRST_POOL_B, POOL_B, LAST_POOL_B, PAIRS - 2):
                    if isinstance(what, int):
                        if norm_next:
                            split(p + 2, par, [what])
                    elif what == "power":
                        if norm_next:
                            group_power(p + 2)
                    elif more:
                        norm_power(p + 1) if what == "norms" else low_product(p + 1, int(what[1]))

            pool.wait_ge(fills, 1)
            for_pairs(pool, step)

        @block.scalar
        def _(act):
            act.dma_start(st_grp, groups).then_inc(c_group, 16)
            act.dma_start(st_id, ident).then_inc(c_group, 16)

            def chunk_value(q, par, c):
                t, g = CHUNKS[c]
                if c == 0:
                    act.wait_ge(norm, (q + 1) * NORM)
                    if isinstance(q, int) and q == 1:
                        act.wait_ge(set_v, 5)
                need(act, l_ok, q * NC_ + c + 1 - XN_RING)
                nc.scalar.activation(xn[:, c % XN_RING, :], xcol(q, t, g * GW, GW), ACT.Identity,
                                     bias=rb[:, par, 1, t:t + 1], scale=rb[:, par, 0, t:t + 1]).then_inc(xn_ok, 1)

            def chunk_high(q, par, c):
                t, g = CHUNKS[c]
                nc.scalar.activation(h_sb[:, par, t, g * GW:g * GW + GW], xcol(q, t, g * GW, GW), ACT.Identity,
                                     bias=rb[:, par, 1, t:t + 1], scale=rb[:, par, 0, t:t + 1]).then_inc(h_ok, 1)

            def split(q, par, what):
                if isinstance(what, int) and CHUNKS[what][0] == 0 and what // 3 < GROUPS - 1:
                    need(act, out_mm, (q - 2) * NO + (what // 3 + 1) * NO // GROUPS)
                if not isinstance(what, str) or what[0] == "x":
                    chunk_value(q, par, int(str(what)[-1]))
                if not isinstance(what, str) or what[0] == "h":
                    chunk_high(q, par, int(str(what)[-1]))

            def to_tok(q, j):
                act.wait_ge(tr_mm, q * SLOTS + j + 1)
                need(act, gram_mm, q * SLOTS + j + 1 - TOK_RING)
                nc.scalar.copy(tok[:, j % TOK_RING, :, :].rearrange("p b n -> p (b n)"), slot_ps(j)
                               ).then_inc(tok_a, 1)

            def spread_norms(q):
                act.wait_ge(rq_mm, q + 1)
                nc.scalar.copy(rq[:, :, :].rearrange("p a c -> p (a c)"), s_ps[0:HC, 0, 0:4 * HC]).then_inc(rq_ok, 1)

            def exp(q):
                act.wait_ge(soft, (q + 1) * SOFT)
                nc.scalar.activation(ez[:, :, :], lz[:, :, :], ACT.Exp).then_inc(exp_ok, 1)

            def high_v(q):
                for b in (0, 1):
                    act.wait_ge(v_mm, 2 * q + b + 1)
                    nc.scalar.copy(vh[:, b, :], s_ps[0:HC, b, 0:2 * C]).then_inc(vh_ok, 1)

            def high_m(q):
                act.wait_ge(m_mm, 2 * q + 1)
                nc.scalar.mul(mh0[:, :, :].rearrange("p b c -> p (b c)"), s_ps[:, 0, 0:2 * C], M_EVAC).then_inc(mh_ok, 1)
                act.wait_ge(m_mm, 2 * q + 2)
                for b in (0, 1):
                    for i in (0, 1):
                        ins = nc.scalar.mul(mh1[C1 * i:C1 * i + C1, b, :], s_ps[C1 * b:C1 * b + C1, 1, 0:C], M_EVAC)
                ins.then_inc(mh_ok, 1)

            def small_gram(q):
                act.wait_ge(gram_mm, (q + 1) * SLOTS)
                for b in (0, 1):
                    nc.scalar.copy(e16[:, b, :], g_ps[:, b, G_C:512]).then_inc(e_ok, 1)

            def high_gram(q):
                for b in (0, 1):
                    act.wait_ge(gfull, 2 * q + b + 1)
                    nc.scalar.copy(q16[:, b, 0, :], g_ps[:, b, 0:256]).then_inc(gh_ok, 1)

            def high_t(q, k):
                src = g_ps[:, k, :] if k < 2 else s_ps[:, 0, :]
                act.wait_ge(t_mm, 3 * q + k + 1)
                nc.scalar.copy(tq[:, k, 0, :], src[:, 0:C]).then_inc(th_ok, 1)

            def high_p(q, k):
                act.wait_ge(pf_ok, 3 * q + k + 1)
                nc.scalar.copy(ph[:, k, :], pf[:, k, :]).then_inc(ph_ok, 1)

            small_steps = {"t0": lambda q: high_t(q, 0), "t1": lambda q: high_t(q, 1), "t2": lambda q: high_t(q, 2),
                           "p0": lambda q: high_p(q, 0), "p1": lambda q: high_p(q, 1), "p2": lambda q: high_p(q, 2),
                           "spread": spread_norms, "exp": exp, "v": high_v, "m": high_m}

            def of_chunk(what):
                return isinstance(what, int) or what[0] in "xh"

            def step(p, par=None, half=None):
                first = isinstance(p, int) and p < 0
                loop = not isinstance(p, int)
                par = p % 2 if not loop else par
                gram, small, norm_next = loop or p + 1 < PAIRS, not first, loop or p + 2 < PAIRS
                for j in (["start"] if first else []) + list(range(SLOTS)):
                    if j != "start" and gram and not slot_is_vector(j):
                        to_tok(p + 1, j)
                    for what in hooks(p, FIRST_ACT_A, ACT_A, LAST_ACT_A, PAIRS - 1).get(j, ()):
                        if first:
                            if str(what)[0] == "z":
                                if what == "z0":
                                    act.wait_ge(norm, NORM)
                                chunk_high(0, 0, int(what[1:]))
                            else:
                                split(1, 1, what)
                        elif of_chunk(what):
                            if gram:
                                split(p + 1, 1 - par, what)
                        elif small:
                            small_steps[what](p)
                if gram:
                    small_gram(p + 1)
                    high_gram(p + 1)
                for what in hooks(p, FIRST_ACT_B, ACT_B, LAST_ACT_B, PAIRS - 2):
                    if of_chunk(what):
                        if norm_next:
                            split(p + 2, par, what)
                    elif gram:
                        small_steps[what](p + 1)

            for_pairs(act, step)

        @block.vector
        def _(dve):
            V = nc.vector
            V.memset(minus_half[:, :], -0.5).then_inc(out_ok, NO)
            V.memset(ones[:, 0:1], 1.0)
            V.memset(ones[0:C1, 1:2], 1.0)
            V.memset(ones[C1:P, 1:2], 0.0)
            V.memset(ones[0:C1, 2:3], 0.0)
            V.memset(ones[C1:P, 2:3], 1.0)
            V.memset(wl1[C1:P, :], 0.0)
            for z in (wkh1, wkl1):
                V.memset(z[C1:P, 0, :], 0.0)
                V.memset(z[0:C1, 1, :], 0.0)
            V.memset(ml1[:, :, :], 0.0).then_inc(fills, 1)
            qk = slice(0, 2 * C)

            def group_constants():
                dve.wait_ge(c_group, 32)
                V.tensor_copy(grp[:, :, :].rearrange("p a m -> p (a m)"), st_grp)
                V.tensor_copy(id16[:, :], st_id)
                V.tensor_copy(id32[:, :], st_id[0:HC, 0:HC]).then_inc(set_v, 1)

            def high_constants():
                dve.wait_ge(c_in, 16 * (8 + NH))
                V.tensor_copy(mask16[:, :], mask[:, :])
                V.tensor_scalar(temp4[:, 0:2], tmp2[:, :], LOGIT_FACTOR, None, ALU.mult)
                V.tensor_scalar(temp4[:, 2:4], tmp2[:, :], LOGIT_FACTOR, None, ALU.mult)
                V.tensor_copy(bias[:, 2:3], bias[:, 0:1])
                V.tensor_scalar(wh0[:, :], w0[:, qk], W_SCALE, None, ALU.mult)
                V.tensor_scalar(wh1[:, :], w1[:, qk], W_SCALE, None, ALU.mult)
                for b in (0, 1):
                    V.tensor_scalar(wkh1[C1 * b:C1 * b + C1, b, :], w1[C1 * b:C1 * b + C1, C:2 * C], W_SCALE, None, ALU.mult)
                V.tensor_scalar(woh[:, :, 0:C], st_wo, W_SCALE, None, ALU.mult)
                V.tensor_scalar(woh[:, :, C:C + P], st_wo[:, :, 0:P], W_SCALE, None, ALU.mult).then_inc(set_v, 1)

            def low_constants():
                dve.wait_ge(set_v, 2)
                dve.wait_ge(fills, 1)

                def low(dst, src, hi):
                    return V.scalar_tensor_tensor(out=dst, in0=src, scalar=W_SCALE, in1=hi, op0=ALU.mult, op1=ALU.subtract)

                low(wl0[:, :], w0[:, qk], wh0[:, :])
                low(wl1[0:C1, :], w1[0:C1, qk], wh1[0:C1, :])
                for b in (0, 1):
                    r = slice(C1 * b, C1 * b + C1)
                    low(wkl1[r, b, :], w1[r, C:2 * C], wkh1[r, b, :])
                low(wol[:, :, 0:C], st_wo, woh[:, :, 0:C])
                low(wol[:, :, C:C + P], st_wo[:, :, 0:P], woh[:, :, C:C + P]).then_inc(set_v, 1)
                dve.wait_ge(wv_tr, 1)
                wv_ps = s_ps[0:HC, 0, 0:2 * C].rearrange("p (j c) -> p j c", j=2)
                V.tensor_scalar(wvh[:, :, :], wv_ps, W_SCALE, None, ALU.mult).then_inc(set_v, 1)
                dve.wait_ge(set_v, 4)
                low(wvl[:, :, :], wv_ps, wvh[:, :, :]).then_inc(set_v, 1)

            def piece(q, par, half, k):
                t, (c, w) = (0, 2, 1)[k // NB], BN[k % NB]
                if k % NB == 0:
                    dve.wait_ge(x_in[t][par], (half + 1) * GROUPS * (32 if t == 1 else 16))
                ins = V.bn_stats(bnst[:, t, 6 * (k % NB):6 * (k % NB) + 6], xcol(q, t, c, w))
                if k % NB == NB - 1:
                    ins.then_inc(bn_done, 1)

            def channel_stats(q):
                dve.wait_ge(bn_done, 3 * q + 3)
                V.memset(msq[:, :], 0.0)
                for t in range(3):
                    V.bn_aggr(mv[:, t, :], bnst[:, t, :]).then_inc(aggr, 1)
                dve.wait_ge(aggr, 3 * q + 3)
                ch = Chain(dve, stat, q * STAT, STAT)
                ch.then(V.tensor_tensor(msq[:, :], mv[:, :, 0], mv[:, :, 0], ALU.mult))
                ch.then(V.tensor_tensor(mv[:, :, 1], mv[:, :, 1], msq[:, :], ALU.add))
                ch.then(V.tensor_copy(parts[:, 0, :, :], mv[:, :, :]))
                ch.then(V.tensor_tensor(res1[:, :, :], mv[:, :, :], parts[:, 0, :, :], ALU.subtract))
                ch.then(V.tensor_copy(parts[:, 1, :, :], res1[:, :, :]))
                ch.then(V.tensor_tensor(parts[:, 2, :, :], res1[:, :, :], parts[:, 1, :, :], ALU.subtract))

            def chunk_value(c):
                t, g = CHUNKS[c]
                if c == 0:
                    dve.wait_ge(norm, NORM)
                need(dve, l_ok, c + 1 - XN_RING)
                V.tensor_scalar(xn[:, c % XN_RING, :], xcol(0, t, g * GW, GW), rb[:, 0, 0, t:t + 1], rb[:, 0, 1, t:t + 1],
                                ALU.mult, ALU.add).then_inc(xn0_ok, 1)

            def group_variance(q, first):
                dve.wait_ge(gn_mm, q + 1)
                ch = Chain(dve, gstep, q * GVAR, GVAR)
                ch.then(V.tensor_reduce(gsum[:, :, :],
                                        sums_ps(first).rearrange("p (t a s) -> p t s a", t=3, a=3),
                                        AX_X, ALU.add))
                ch.then(V.tensor_scalar(gsum[:, :, :], gsum[:, :, :], 1 / CG, None, ALU.mult))
                ch.then(V.tensor_tensor(gvar[:, :], gsum[:, :, 0], gsum[:, :, 0], ALU.mult))
                ch.then(V.tensor_tensor(gvar[:, :], gsum[:, :, 1], gvar[:, :], ALU.subtract))
                dve.wait_ge(gstep, (q + 1) * GVAR)
                V.tensor_scalar(gvar[:, :], gvar[:, :], GN_EPS, GN_EPS, ALU.add, ALU.max).then_inc(var_ok, 1)

            def scale_shift(q, par):
                dve.wait_ge(grs_ok, q + 1)
                need(dve, h_ok, (q - 1) * NC_)
                ch = Chain(dve, norm, q * NORM, NORM)
                ch.then(V.tensor_scalar(rb[:, par, 0, :], grs[:, :], X_SCALE, None, ALU.mult))
                ch.then(V.scalar_tensor_tensor(out=rb[:, par, 1, :], in0=gsum[:, :, 0], scalar=-1.0, in1=rb[:, par, 0, :],
                                               op0=ALU.mult, op1=ALU.mult))

            def to_tok(q, j):
                dve.wait_ge(tr_mm, q * SLOTS + j + 1)
                need(dve, gram_mm, q * SLOTS + j + 1 - TOK_RING)
                V.tensor_copy(tok[:, j % TOK_RING, :, :].rearrange("p b n -> p (b n)"), slot_ps(j)
                              ).then_inc(tok_v, 1)

            def norms(q):
                dve.wait_ge(nrm_mm, q + 1)
                V.tensor_scalar(n8[:, :], s_ps[0:HC, 0, 0:8], NORM_EPS ** 2 * NORM_FACTOR, None, ALU.max
                                ).then_inc(n8_ok, 1)

            def diagonals(q):
                dve.wait_ge(r8_ok, q + 1)
                V.tensor_tensor(dq[:, :, :], r8[:, 4:8].unsqueeze(2).to_broadcast([HC, 4, HC]),
                                id32[:, :].unsqueeze(1).to_broadcast([HC, 4, HC]), ALU.mult).then_inc(dq_ok, 1)
                V.tensor_tensor(rk[:, :], r8[:, 0:4], temp4[:, :], ALU.mult).then_inc(rk_ok, 1)

            def softmax_in(q):
                dve.wait_ge(rq_ok, q + 1)
                dve.wait_ge(s_mm, q + 1)
                dve.wait_ge(rk_ok, q + 1)
                ch = Chain(dve, soft, q * SOFT, SOFT)
                ch.then(V.tensor_tensor(lg[:, :, :].rearrange("p a c -> p (a c)"), s_ps[0:HC, 1, 0:4 * HC],
                                        rq[:, :, :].rearrange("p a c -> p (a c)"), ALU.mult))
                ch.then(V.tensor_reduce(lz[:, :, :], lg[:, :, :].rearrange("p a (g d) -> p a d g", g=NH), AX_X, ALU.add))
                ch.then(V.tensor_tensor(lz[:, :, :], lz[:, :, :], rk[:, :].unsqueeze(2).to_broadcast([HC, 4, D]), ALU.mult))
                ch.then(V.tensor_reduce(mx[:, :], lz[:, :, :], AX_X, ALU.max))
                ch.then(V.tensor_tensor(lz[:, :, :], lz[:, :, :], mx[:, :].unsqueeze(2).to_broadcast([HC, 4, D]),
                                        ALU.subtract))

            def softmax_out(q):
                dve.wait_ge(exp_ok, q + 1)
                ch = Chain(dve, attn, q * ATTN, ATTN)
                ch.then(V.tensor_reduce(sm[:, :], ez[:, :, :], AX_X, ALU.add))
                ch.then(V.reciprocal(sm[:, :], sm[:, :]))
                ch.then(V.scalar_tensor_tensor(out=lz[:, :, :], in0=ez[:, :, :], scalar=A_SCALE,
                                               in1=sm[:, :].unsqueeze(2).to_broadcast([HC, 4, D]),
                                               op0=ALU.mult, op1=ALU.mult))
                V.tensor_copy(a16[:, 0, :, :], lz[:, :, :]).then_inc(attn_s, 1)
                dve.wait_ge(attn_s, 2 * q + 1)
                V.tensor_tensor(a16[:, 1, :, :], lz[:, :, :], a16[:, 0, :, :], ALU.subtract).then_inc(attn_s, 1)
                dve.wait_ge(attn_s, 2 * q + 2)
                m4 = mask16[:, :].rearrange("p (g d) -> p g d", g=NH)
                for i in (0, 1):
                    for a in range(4):
                        ins = V.tensor_tensor(ax[:, i, a, :, :], a16[:, i, a, :].unsqueeze(1).to_broadcast([HC, NH, D]),
                                              m4, ALU.mult)
                    ch.then(ins)

            def low_v(q):
                for b in (0, 1):
                    dve.wait_ge(vh_ok, 2 * q + b + 1)
                    V.tensor_tensor(vl[:, b, :], s_ps[0:HC, b, 0:2 * C], vh[:, b, :], ALU.subtract).then_inc(vl_ok, 1)

            def low_m(q):
                def lowm(dst, src, hi):
                    return V.scalar_tensor_tensor(out=dst, in0=src, scalar=M_EVAC, in1=hi, op0=ALU.mult, op1=ALU.subtract)
                dve.wait_ge(mh_ok, 2 * q + 1)
                lowm(ml0[:, :, :].rearrange("p b c -> p (b c)"), s_ps[:, 0, 0:2 * C],
                     mh0[:, :, :].rearrange("p b c -> p (b c)")).then_inc(ml_ok, 1)
                dve.wait_ge(mh_ok, 2 * q + 2)
                l1 = ml1[:, :, :].rearrange("p t c -> p (t c)")
                lowm(l1[0:C1, 0:C], s_ps[0:C1, 1, 0:C], mh1[0:C1, 0, :])
                lowm(l1[C1:P, C:2 * C], s_ps[C1:P, 1, 0:C], mh1[C1:P, 1, :]).then_inc(ml_ok, 1)

            def low_gram(q):
                for b in (0, 1):
                    dve.wait_ge(gh_ok, 2 * q + b + 1)
                    V.tensor_tensor(q16[:, b, 1, :], g_ps[:, b, 0:256], q16[:, b, 0, :], ALU.subtract
                                    ).then_inc(gl_ok, 1)

            def z_copy(q):
                dve.wait_ge(z_mm, q + 1)
                V.tensor_copy(z16[:, :, :].rearrange("p b c -> p (b c)"), z_ps).then_inc(z_ok, 1)

            def low_t(q, k):
                src = g_ps[:, k, :] if k < 2 else s_ps[:, 0, :]
                dve.wait_ge(th_ok, 3 * q + k + 1)
                w = (w0 if k < 2 else w1)[:, qk]
                V.tensor_tensor(pf[:, k, :], src[:, 0:2 * C], w, ALU.mult).then_inc(pf_ok, 1)
                V.tensor_tensor(tq[:, k, 1, :], src[:, 0:C], tq[:, k, 0, :], ALU.subtract).then_inc(tl_ok, 1)

            def result(q, n):
                (t, c), w = OUTS[n], BW
                dve.wait_ge(out_mm, q * NO + n + 1)
                xs = xcol(q, t, c, w)
                V.scalar_tensor_tensor(out=xs, in0=block_ps(n), scalar=bias[:, t:t + 1], in1=xs,
                                       op0=ALU.add, op1=ALU.add).then_inc(out_ok, 1)

            small_steps = {"gram": low_gram, "z": z_copy, "t0": lambda q: low_t(q, 0), "t1": lambda q: low_t(q, 1),
                           "t2": lambda q: low_t(q, 2), "norms": norms, "diag": diagonals, "soft_in": softmax_in,
                           "soft_out": softmax_out, "v": low_v, "m": low_m}

            def step(p, par=None, half=None):
                first = isinstance(p, int) and p < 0
                loop = not isinstance(p, int)
                if not loop:
                    par, half = p % 2, p // 2
                if first:
                    for k in range(3 * NB):
                        piece(0, 0, 0, k)
                        if k == NB - 1:
                            group_constants()
                    channel_stats(0)
                    group_variance(0, True)
                    scale_shift(0, 0)
                gram, small, norm_next = loop or p + 1 < PAIRS, not first, loop or p + 2 < PAIRS
                pieces = list(range(3 * NB)) if norm_next else []

                def partial(count):
                    for _ in range(count if pieces else 0):
                        piece(p + 2, par, half + 1, pieces.pop(0))

                def first_step(what):
                    if what[0] == "z":
                        chunk_value(int(what[1:]))
                    elif what == "bn":
                        partial(1)
                    else:
                        {"high": high_constants, "low": low_constants}[what]()

                for what in FIRST_VEC_A["start"] if first else ():
                    first_step(what)

                def norm_step(what):
                    if what == "scale":
                        scale_shift(p + 2, par)
                    elif what == "var":
                        group_variance(p + 2, first)
                    else:
                        channel_stats(p + 2)

                for j in range(SLOTS):
                    if gram and slot_is_vector(j):
                        to_tok(p + 1, j)
                    for what in hooks(p, FIRST_VEC_A, VEC_A, LAST_VEC_A, PAIRS - 1).get(j, ()):
                        if what in ("stats", "var", "scale"):
                            if norm_next:
                                norm_step(what)
                        elif first:
                            first_step(what)
                        elif small:
                            small_steps[what](p)
                    partial(0 if first else BN_A.get(j, 0))
                for n in range(NO):
                    if small:
                        result(p, n)
                    for what in hooks(p, FIRST_VEC_B, VEC_B, LAST_VEC_B, PAIRS - 2).get(n, ()):
                        if what in ("stats", "var", "scale"):
                            if norm_next:
                                norm_step(what)
                        elif gram:
                            small_steps[what](p + 1)
                    partial(0 if first else BN_B.get(n, 0))
                assert not pieces

            for_pairs(dve, step)

        @block.tensor
        def _(pe):
            def mm(dst, lhs, rhs, start, stop=False):
                return nc.tensor.matmul(dst, lhs, rhs, start=start, stop=stop, skip_group_check=True)

            def transpose_wv():
                pe.wait_ge(c_in, 16 * (8 + NH))
                for j in (0, 1):
                    cols = slice(2 * C + HC * j, 2 * C + HC * j + HC)
                    nc.tensor.transpose(s_ps[0:HC, 0, C * j:C * j + P], w0[:, cols], st_id)
                    last = nc.tensor.transpose(s_ps[0:HC, 0, C * j + P:C * j + C], w1[0:C1, cols], st_id[0:C1, 0:C1])
                last.then_inc(wv_tr, 1)

            def group_sums(q, first):
                pe.wait_ge(stat, (q + 1) * STAT)
                if not first:
                    pe.wait_ge(out_ok, (q - 1) * NO + SUMS_AT)
                dst_ps = sums_ps(first)
                for dst, srcs in ((0, ((0, 0), (1, 4))), (1, ((1, 1), (0, 2), (2, 3))), (2, ((2, 0), (1, 5)))):
                    for k, (src, g) in enumerate(srcs):
                        last = mm(dst_ps[:, 6 * dst:6 * dst + 6], grp[:, g, :],
                                  parts[:, :, src, :], k == 0, k == len(srcs) - 1)
                last.then_inc(gn_mm, 1)

            def in_tok(q, j):
                before = sum(slot_is_vector(k) for k in range(j))
                if slot_is_vector(j):
                    pe.wait_ge(tok_v, q * NV + before + 1)
                else:
                    pe.wait_ge(tok_a, q * NA + j - before + 1)

            def transposes(q, par, j):
                if j < RING:
                    need(pe, out_ok, (q - 1) * NO + NO - RING + j + 1)
                else:
                    in_tok(q, j - RING)
                if j * P % GW == 0:
                    pe.wait_ge(h_ok, q * NC_ + 3 * (j * P // GW) + 3)
                    pe.wait_ge(l_ok, q * NC_ + 3 * (j * P // GW) + 3)
                bank = slot_ps(j).rearrange("p (b n) -> p b n", b=2)
                px = slice(P * j, P * j + P)
                for b in (0, 1):
                    nc.tensor.transpose(bank[:, b, 0:P], h_sb[:, par, 2 * b, px], id16[:, :])
                    nc.tensor.transpose(bank[:, b, 256:384], l_sb[:, par, 2 * b, px], id16[:, :])
                nc.tensor.transpose(bank[:, :, P:P + C1], h_sb[:, par, 1, px], id16[:, :])
                nc.tensor.transpose(bank[:, :, P + C1:P + 2 * C1], l_sb[:, par, 1, px], id16[:, :]).then_inc(tr_mm, 1)

            def gram(q, j):
                in_tok(q, j)
                if j == 0:
                    need(pe, tl_ok, 3 * q)
                    need(pe, pf_ok, 3 * q)
                first, end = j == 0, j == SLOTS - 1
                for b in (0, 1):
                    s = tok[:, j % TOK_RING, b, :]
                    bank = g_ps[:, b, :]
                    mm(bank.rearrange("p (r c) -> p r c", r=2)[:, :, 0:C], s[:, 0:P], s[:, 0:384], first)
                    mm(bank[:, G_C:G_C + C1], s[:, P:256], s[:, P:C], False)
                    last = mm(bank[:, G_B:G_B + C1], s[:, 256:384], s[:, P:C], False)
                last.then_inc(gram_mm, 1)

            def finish_gram(q):
                for b in (0, 1):
                    pe.wait_ge(e_ok, 2 * q + b + 1)
                    bank, e = g_ps[:, b, :], e16[:, b, :]
                    mm(bank[:, 0:P], e[:, 128:256], id16[:, :], False)
                    mm(bank[:, 0:P], id16[:, :], e[:, 128:256], False)
                    mm(bank[:, P:C], id16[:, :], e[:, 64:128], False)
                    mm(bank[:, P:C], id16[:, :], e[:, 256:320], False)
                    mm(bank[0:C1, G_C:G_C + C1], e[C1:P, 0:C1], id16[C1:P, C1:P], False)
                    mm(bank[0:C1, G_C:G_C + C1], id16[C1:P, C1:P], e[C1:P, 0:C1], False, True).then_inc(gfull, 1)

            def gram_weights(q, ready):
                z = z16
                if not ready:
                    pe.wait_ge(gl_ok, 2 * q + 2)
                else:
                    pe.wait_ge(z_ok, q + 1)
                for b in (0, 1):
                    dst = g_ps[:, b, 0:2 * C]
                    hi, lo = (q16[:, b, i, 0:P] for i in (0, 1))
                    if not ready:
                        mm(dst, hi, wh0[:, :], True)
                        mm(dst, hi, wl0[:, :], False)
                        mm(dst, lo, wh0[:, :], False)
                    else:
                        mm(dst, z[:, b, 0:P], wh1[:, :], False)
                        mm(dst, z[:, b, 0:P], wl1[:, :], False, True).then_inc(t_mm, 1)
                if not ready:
                    need(pe, ml_ok, 2 * q)
                for k in (range(3, 5) if ready else range(3)):
                    for b in (0, 1):
                        dst = s_ps[C1 * b:C1 * b + C1, 0, 0:2 * C]
                        hi, lo = (q16[:, b, i, P:C] for i in (0, 1))
                        lhs, rhs = ((hi, wh0), (hi, wl0), (lo, wh0), (z[:, b, P:C], wh1), (z[:, b, P:C], wl1))[k]
                        last = mm(dst, lhs, rhs[:, :], k == 0, k == 4)
                if ready:
                    last.then_inc(t_mm, 1)
                    return
                for b in (0, 1):
                    for i in (0, 1):
                        rows = slice(C1 * i, C1 * i + C1)
                        nc.tensor.transpose(z_ps[rows, C * b:C * b + P], q16[:, b, i, P:C], id16[:, :])
                        last = nc.tensor.transpose(z_ps[rows, C * b + P:C * b + C], q16[0:C1, b, i, C:256],
                                                   id16[0:C1, 0:C1])
                last.then_inc(z_mm, 1)

            def norms(q):
                pe.wait_ge(ph_ok, 3 * q + 3)
                pe.wait_ge(pl_ok, 3 * q + 3)
                pe.wait_ge(tl_ok, 3 * q + 3)
                for m in range(8):
                    b, j = m // 2 % 2, m % 2
                    cols = slice((C if m < 4 else 0) + HC * j, (C if m < 4 else 0) + HC * j + HC)
                    terms = [(ph[:, b, cols], 0), (pl[:, b, cols], 0), (ph[:, 2, cols], 1 + b), (pl[:, 2, cols], 1 + b)]
                    for k, (lhs, o) in enumerate(terms):
                        last = mm(s_ps[0:HC, 0, m:m + 1], lhs, ones[:, o:o + 1], k == 0, k == 3)
                last.then_inc(nrm_mm, 1)

            def scores(q):
                pe.wait_ge(tl_ok, 3 * q + 3)
                for b in (0, 1):
                    for j in (0, 1):
                        kc = slice(HC * j, HC * j + HC)
                        wk = slice(C + HC * j, C + HC * j + HC)
                        dst = s_ps[0:HC, 1, HC * (2 * b + j):HC * (2 * b + j) + HC]
                        terms = [(wh0[:, wk], tq[:, b, 0, kc]), (wh0[:, wk], tq[:, b, 1, kc]), (wl0[:, wk], tq[:, b, 0, kc]),
                                 (wkh1[:, b, kc], tq[:, 2, 0, kc]), (wkh1[:, b, kc], tq[:, 2, 1, kc]),
                                 (wkl1[:, b, kc], tq[:, 2, 0, kc])]
                        for k, (lhs, rhs) in enumerate(terms):
                            last = mm(dst, lhs, rhs, k == 0, k == 5)
                last.then_inc(s_mm, 1)

            def spread_norms(q):
                pe.wait_ge(dq_ok, q + 1)
                mm(s_ps[0:HC, 0, 0:4 * HC], mask[:, :], dq[:, :, :].rearrange("p a c -> p (a c)"), True, True
                   ).then_inc(rq_mm, 1)

            def attn_values(q):
                pe.wait_ge(attn, (q + 1) * ATTN)
                for b in (0, 1):
                    for j in (0, 1):
                        a_hi, a_lo = (ax[:, i, 2 * b + j, :, :].rearrange("p g d -> p (g d)") for i in (0, 1))
                        dst = s_ps[0:HC, b, C * j:C * j + C]
                        mm(dst, a_hi, wvh[:, j, :], True)
                        mm(dst, a_hi, wvl[:, j, :], False)
                        last = mm(dst, a_lo, wvh[:, j, :], False, True)
                    last.then_inc(v_mm, 1)

            def folded_weights(q):
                pe.wait_ge(vl_ok, 2 * q + 2)
                for b in (0, 1):
                    for j in (0, 1):
                        c0 = C * j
                        dst = s_ps[:, 0, C * b:C * b + C]
                        mm(dst, vh[:, b, c0:c0 + P], woh[:, j, 0:C], j == 0)
                        mm(dst, vh[:, b, c0:c0 + P], wol[:, j, 0:C], False)
                        last = mm(dst, vl[:, b, c0:c0 + P], woh[:, j, 0:C], False, j == 1)
                last.then_inc(m_mm, 1)
                for j in (0, 1):
                    for k in range(3):
                        for b in (0, 1):
                            v, wo = ((vh, woh), (vh, wol), (vl, woh))[k]
                            last = mm(s_ps[C1 * b:C1 * b + C1, 1, 0:C], v[:, b, C * j + P:C * j + C],
                                      wo[:, j, P * b:P * b + C], j == 0 and k == 0, j == 1 and k == 2)
                last.then_inc(m_mm, 1)

            def result(q, par, n, sums):
                (t, c), w = OUTS[n], BW
                if n == 0:
                    pe.wait_ge(ml_ok, 2 * q + 2)
                if n >= RING:
                    pe.wait_ge(out_ok, (q + 1) * NO + n - RING + 1)
                elif isinstance(q, int) and q == PAIRS - 1:
                    pe.wait_ge(out_ok, q * NO + NO - RING + (n + SLOTS) % RING + 1)
                if sums:
                    pe.wait_ge(gstep, (q + 2) * GVAR + 1)
                if n % (NO // GROUPS) == 0:
                    pe.wait_ge(hl_in[n // (NO // GROUPS)], (q + 1) * 64)
                dst = block_ps(n)
                h, l = (a[:, par, :, c:c + w] for a in (h_sb, l_sb))
                if t != 1:
                    b = t // 2
                    mm(dst, mh0[:, b, 0:P], h[:, t, :], True)
                    mm(dst, mh0[:, b, 0:P], l[:, t, :], False)
                    mm(dst, mh1[:, b, C1 * b:C1 * b + P], hl[:, b, c:c + w], False)
                    mm(dst, ml0[:, b, 0:P], h[:, t, :], False)
                    mm(dst, ml1[:, t, :], h[:, 1, :], False, True).then_inc(out_mm, 1)
                else:
                    mm(dst, ml1[:, 1, :], h[:, 1, :], True)
                    for b in (0, 1):
                        mm(dst[C1 * b:C1 * b + C1, :], mh1[:, b, P - P * b:C - P * b], hl[:, b, c:c + w], False)
                    for k, (m, a) in enumerate(((mh0, h), (mh0, l), (ml0, h))):
                        for b in (0, 1):
                            last = mm(dst[C1 * b:C1 * b + C1, :], m[:, b, P:C], a[:, 2 * b, :], False, k == 2)
                    last.then_inc(out_mm, 1)

            small_steps = {"gram": finish_gram, "w0": lambda q: gram_weights(q, False),
                           "w1": lambda q: gram_weights(q, True), "scores": scores, "norms": norms,
                           "spread": spread_norms, "v": attn_values, "m": folded_weights}

            def step(p, par=None, half=None):
                first = isinstance(p, int) and p < 0
                loop = not isinstance(p, int)
                par = p % 2 if not loop else par
                if first:
                    pe.wait_ge(set_v, 1)
                    group_sums(0, True)
                    transpose_wv()
                more, small, norm_next = loop or p + 1 < PAIRS, not first, loop or p + 2 < PAIRS
                if more:
                    for j in range(AHEAD):
                        transposes(p + 1, 1 - par, j)
                for j in range(SLOTS):
                    if more:
                        gram(p + 1, j)
                        if j + AHEAD < SLOTS:
                            transposes(p + 1, 1 - par, j + AHEAD)
                    for what in hooks(p, FIRST_PE_A, PE_A, LAST_PE_A, PAIRS - 1).get(j, ()):
                        if what == "sums":
                            if norm_next:
                                group_sums(p + 2, first)
                        elif small:
                            small_steps[what](p)
                if first:
                    pe.wait_ge(set_v, 5)
                    pe.wait_ge(fills, 1)
                for n in range(NO):
                    if small:
                        result(p, par, n, norm_next and n == SUMS_AT + 3)
                    for what in hooks(p, FIRST_PE_B, PE_B, LAST_PE_B, PAIRS - 2).get(n, ()):
                        if what == "sums":
                            if norm_next:
                                group_sums(p + 2, first)
                        elif more:
                            small_steps[what](p + 1)

            for_pairs(pe, step)


def constants():
    C, C1 = 192, 64
    channel = [np.arange(P), P + np.arange(P) % C1, np.arange(P)]
    image = [np.zeros(P, int), np.arange(P) // C1, np.ones(P, int)]
    grp = np.zeros((P, 6, P), np.float32)
    for n, (src, dst) in enumerate(((0, 0), (1, 1), (0, 1), (2, 1), (1, 0), (1, 2))):
        grp[:, n, :] = ((channel[src] // CG)[:, None] == (channel[dst] // CG)[None]) & \
            (image[src][:, None] == image[dst][None])
    head = np.arange(C // 2) // (C // HEADS)
    return {"ident": np.eye(P, dtype=np.float32), "groups": grp.reshape(P, 6 * P),
            "headmask": (head[:, None] == head[None]).astype(np.float32)}


_INS = ['x', 'L0_conv_w_qkv', 'L0_conv_temperature', 'L0_conv_w_out', 'L0_conv_b_out']
_OUTS = [((16, 192, 48, 48), 'float32')]


def kernel(**inputs):
    import numpy as _np
    import concourse.bacc as _bacc
    from concourse import mybir as _mybir
    from concourse.bass_utils import run_bass_kernel_spmd as _run

    nc = _bacc.Bacc("TRN2", target_bir_lowering=False, num_devices=1)
    arrays, args = {}, []
    given = {name: _np.ascontiguousarray(inputs[name]) for name in _INS}
    given.update(constants())
    for name, a in given.items():
        arrays[f"in_{name}_dram"] = a
        args.append(nc.dram_tensor(f"in_{name}_dram", a.shape, _mybir.dt.from_np(a.dtype), kind="ExternalInput").ap())
    for i, (shape, dtype) in enumerate(_OUTS):
        dt = _mybir.dt.from_np(_np.dtype(dtype))
        args.append(nc.dram_tensor(f"out_{i}_dram", shape, dt, kind="ExternalOutput").ap())
    preact_attention(nc, *args)
    r = _run(nc, [arrays], core_ids=[0])
    got = tuple(r.results[0][f"out_{i}_dram"] for i in range(len(_OUTS)))
    return got[0]
```
